# Optimizing a Trainium2 kernel written in Bass

```python
import numpy as np
import jax
import jax.numpy as jnp

def _softmax(x, axis=-1):
    return jax.nn.softmax(x, axis=axis)

def _gelu(x):
    return jax.nn.gelu(x, approximate=True)

def _silu(x):
    return jax.nn.silu(x)

def _sigmoid(x):
    return jax.nn.sigmoid(x)

def _layernorm(x, axis=-1, eps=1e-05):
    m = jnp.mean(x, axis=axis, keepdims=True)
    v = jnp.var(x, axis=axis, keepdims=True)
    return (x - m) / jnp.sqrt(v + eps)

def _scatter_add(tgt, idx, src, axis=0):
    return tgt.at[idx].add(src)

def _segment_sum(src, seg, n):
    return jax.ops.segment_sum(src, seg, n)
kernel_name = 'mk_conv_preact_d4_conv_nhwc64_r2_331e58'

def setup_inputs(seed: int=0):
    np.random.seed(seed)
    _w = jnp.asarray

    def _rec_inputs():
        import jax
        import jax.numpy as jnp
        _gk = jax.random.key(seed)
        x = -0.000125 + 0.9999 * jax.random.normal(jax.random.fold_in(_gk, 1), (8, 128, 128, 32), jnp.float32)
        return x
    x = _rec_inputs()

    def _L0_conv_setup():
        import jax, jax.numpy as jnp
        import numpy as np
        DIM, MULTI = (32, 4)
        B, H, W = (8, 128, 128)

        def _gelu(t):
            return jax.nn.gelu(t, approximate=False)
        key = jax.random.key(seed)
        k0, k1, k2, k3 = jax.random.split(key, 4)
        x = jax.random.normal(k0, (B, H, W, DIM), dtype=jnp.float32)
        w1 = jax.random.normal(k1, (DIM, MULTI), dtype=jnp.float32)
        wg = jax.random.normal(k2, (MULTI, DIM, DIM), dtype=jnp.float32) / np.float32(np.sqrt(DIM))
        w2 = jax.random.normal(k3, (DIM, MULTI), dtype=jnp.float32) / np.float32(np.sqrt(MULTI))
        return {'x': x, 'w1': w1, 'wg': wg, 'w2': w2}
    _L0_conv_all = _L0_conv_setup()
    _L0_conv_in = {k: v for k, v in _L0_conv_all.items() if k in ('w1', 'wg', 'w2')}
    del _L0_conv_all

    def _L1_conv_setup():
        import jax, jax.numpy as jnp
        import numpy as np
        from jax import lax

        def make_fir_kernel():
            k1 = np.array([1.0, 3.0, 3.0, 1.0], np.float32)
            k2 = np.outer(k1, k1)
            k2 /= np.sum(np.abs(k2))
            return k2.astype(np.float32)
        key = jax.random.key(seed)
        x = jax.random.normal(key, (16, 128, 128, 32), dtype=jnp.float32)
        kernel = jnp.asarray(make_fir_kernel())
        return {'x': x, 'kernel': kernel}
    _L1_conv_all = _L1_conv_setup()
    _L1_conv_in = {k: v for k, v in _L1_conv_all.items() if k in ('kernel',)}
    del _L1_conv_all

    def _L2_conv_setup():
        import jax, jax.numpy as jnp
        import numpy as np
        DIM = 32
        OUT_DIM = 32
        HEADS = 4
        WS = 8
        N = WS * WS
        QK_OUT = N * HEADS + OUT_DIM
        key = jax.random.key(seed)
        k1, k2, k3 = jax.random.split(key, 3)
        x = jax.random.normal(k1, (8, 128, 128, DIM), dtype=jnp.float32)
        W_qk = jax.random.normal(k2, (QK_OUT, DIM), dtype=jnp.float32) * (1.0 / np.sqrt(DIM))
        b_qk = jax.random.normal(k3, (QK_OUT,), dtype=jnp.float32) * 0.01
        temperature = jnp.full((HEADS,), 1.0 / np.sqrt(DIM), dtype=jnp.float32)
        return {'x': x, 'W_qk': W_qk, 'b_qk': b_qk, 'temperature': temperature}
    _L2_conv_all = _L2_conv_setup()
    _L2_conv_in = {k: v for k, v in _L2_conv_all.items() if k in ('W_qk', 'b_qk', 'temperature')}
    del _L2_conv_all

    def _L3_conv_setup():
        import jax, jax.numpy as jnp
        import numpy as np
        BN_EPS = 0.001
        LEAKY_ALPHA = 0.3
        K = 3
        S = 1
        key = jax.random.key(seed)
        k1, k2 = jax.random.split(key)
        B, H, W, C = (16, 64, 64, 32)
        inputs = jax.random.normal(k1, (B, H, W, C), dtype=jnp.float32)
        W1 = jax.random.normal(k2, (C, K * K), dtype=jnp.float32) * (1.0 / np.sqrt(C))
        b1 = jnp.zeros((K * K,), dtype=jnp.float32)
        gamma = jnp.ones((C,), dtype=jnp.float32)
        beta = jnp.zeros((C,), dtype=jnp.float32)
        return {'inputs': inputs, 'W1': W1, 'b1': b1, 'gamma': gamma, 'beta': beta}
    _L3_conv_all = _L3_conv_setup()
    _L3_conv_in = {k: v for k, v in _L3_conv_all.items() if k in ('W1', 'b1', 'gamma', 'beta')}
    del _L3_conv_all
    return {'x': x, 'L0_conv_w1': _L0_conv_in['w1'], 'L0_conv_wg': _L0_conv_in['wg'], 'L0_conv_w2': _L0_conv_in['w2'], 'L1_conv_kernel': _L1_conv_in['kernel'], 'L2_conv_W_qk': _L2_conv_in['W_qk'], 'L2_conv_b_qk': _L2_conv_in['b_qk'], 'L2_conv_temperature': _L2_conv_in['temperature'], 'L3_conv_W1': _L3_conv_in['W1'], 'L3_conv_b1': _L3_conv_in['b1'], 'L3_conv_gamma': _L3_conv_in['gamma'], 'L3_conv_beta': _L3_conv_in['beta']}

def reference(x, L0_conv_w1, L0_conv_wg, L0_conv_w2, L1_conv_kernel, L2_conv_W_qk, L2_conv_b_qk, L2_conv_temperature, L3_conv_W1, L3_conv_b1, L3_conv_gamma, L3_conv_beta):
    import jax
    import jax.numpy as jnp

    def _L0_conv_ref(x, w1, wg, w2):
        import jax, jax.numpy as jnp
        import numpy as np
        DIM, MULTI = (32, 4)
        B, H, W = (8, 128, 128)

        def _gelu(t):
            return jax.nn.gelu(t, approximate=False)
        y = _gelu(x[..., :, None] * w1)
        z = _gelu(jnp.einsum('bhwim,moi->bhwmo', y, wg))
        out = jnp.einsum('bhwmc,cm->bhwc', z, w2)
        return out

    def _L1_conv_ref(x, kernel):
        import jax, jax.numpy as jnp
        import numpy as np
        from jax import lax

        def make_fir_kernel():
            k1 = np.array([1.0, 3.0, 3.0, 1.0], np.float32)
            k2 = np.outer(k1, k1)
            k2 /= np.sum(np.abs(k2))
            return k2.astype(np.float32)
        C = x.shape[-1]
        xp = jnp.pad(x, ((0, 0), (1, 2), (1, 2), (0, 0)))
        w = jnp.tile(kernel[:, :, None, None], (1, 1, 1, C))
        out = lax.conv_general_dilated(xp, w, window_strides=(1, 1), padding='VALID', dimension_numbers=('NHWC', 'HWIO', 'NHWC'), feature_group_count=C)
        return out

    def _L2_conv_ref(x, W_qk, b_qk, temperature):
        import jax, jax.numpy as jnp
        import numpy as np
        DIM = 32
        OUT_DIM = 32
        HEADS = 4
        WS = 8
        N = WS * WS
        QK_OUT = N * HEADS + OUT_DIM
        B, H, W, _ = x.shape
        qk = jnp.einsum('bhwc,oc->bhwo', x, W_qk) + b_qk
        pad_h = -H % WS
        pad_w = -W % WS
        qk = jnp.pad(qk, ((0, 0), (0, pad_h), (0, pad_w), (0, 0)))
        Hp, Wp = (H + pad_h, W + pad_w)
        H1, W1 = (Hp // WS, Wp // WS)
        ck = OUT_DIM // HEADS
        q = qk[..., :N * HEADS]
        k = qk[..., N * HEADS:]
        q = q.reshape(B, WS, H1, WS, W1, HEADS, N)
        q = q.transpose(0, 2, 4, 5, 6, 1, 3).reshape(B, H1, W1, HEADS, N, WS * WS)
        k = k.reshape(B, WS, H1, WS, W1, HEADS, ck)
        k = k.transpose(0, 2, 4, 5, 6, 1, 3).reshape(B, H1, W1, HEADS, ck, WS * WS)
        attn = jnp.einsum('bxyhcp,bxyhdp->bxyhcd', q, k)
        attn = attn * temperature[None, None, None, :, None, None]
        out = attn.reshape(B, H1, W1, HEADS, WS, WS, ck)
        out = out.transpose(0, 3, 6, 1, 4, 2, 5).reshape(B, HEADS * ck, H1 * WS, W1 * WS)
        out = out[:, :, :H, :W]
        return out.transpose(0, 2, 3, 1)

    def _L3_conv_ref(inputs, W1, b1, gamma, beta):
        import jax, jax.numpy as jnp
        import numpy as np
        BN_EPS = 0.001
        LEAKY_ALPHA = 0.3
        K = 3
        S = 1
        B, H, W, C = inputs.shape
        nH = (H - K) // S + 1
        nW = (W - K) // S + 1
        ci = jnp.arange(nH) * S + K // 2
        cj = jnp.arange(nW) * S + K // 2
        centers = inputs[:, ci][:, :, cj]
        kernel = centers @ W1 + b1
        kernel = kernel.reshape(B, nH, nW, K, K, 1)
        hi = jnp.arange(nH)[:, None] * S + jnp.arange(K)[None, :]
        wi = jnp.arange(nW)[:, None] * S + jnp.arange(K)[None, :]
        patches = inputs[:, hi]
        patches = patches[:, :, :, wi]
        patches = patches.transpose(0, 1, 3, 2, 4, 5)
        weighted = patches * kernel
        yout = jnp.zeros_like(inputs).at[:, hi[:, None, :, None], wi[None, :, None, :], :].add(weighted)
        mean = jnp.mean(yout, axis=(0, 1, 2))
        var = jnp.var(yout, axis=(0, 1, 2))
        yn = (yout - mean) * jax.lax.rsqrt(var + BN_EPS) * gamma + beta
        return jnp.where(yn >= 0, yn, LEAKY_ALPHA * yn)

    def _gn(v, G=32, eps=1e-05):
        B_, H_, W_, C_ = v.shape
        g = v.reshape(B_, H_, W_, G, C_ // G)
        m = jnp.mean(g, axis=(1, 2, 4), keepdims=True)
        s = jnp.var(g, axis=(1, 2, 4), keepdims=True)
        return ((g - m) / jnp.sqrt(s + eps)).reshape(v.shape)

    def _ln_c(v, eps=1e-06):
        m = jnp.mean(v, axis=-1, keepdims=True)
        s = jnp.var(v, axis=-1, keepdims=True)
        return (v - m) / jnp.sqrt(s + eps)

    def _ln_t(v, eps=1e-05):
        m = jnp.mean(v, axis=-1, keepdims=True)
        s = jnp.var(v, axis=-1, keepdims=True)
        return (v - m) / jnp.sqrt(s + eps)

    def _to_tokens(v):
        B_, H_, W_, C_ = v.shape
        return v.reshape(B_, H_ * W_, C_)

    def _from_tokens(t, like):
        return t.reshape(like.shape)
    x = x + _L0_conv_ref(_gn(x), L0_conv_w1, L0_conv_wg, L0_conv_w2)
    x = x + _L1_conv_ref(_gn(x), L1_conv_kernel)
    x = x + _L2_conv_ref(_gn(x), L2_conv_W_qk, L2_conv_b_qk, L2_conv_temperature)
    x = x + _L3_conv_ref(_gn(x), L3_conv_W1, L3_conv_b1, L3_conv_gamma, L3_conv_beta)
    return x

_drawn_inputs = setup_inputs


def setup_inputs(seed=0):
    import zlib

    import numpy as np

    out = dict(_drawn_inputs(seed))
    spreads = {'L2_conv_temperature': (0.1767766922712326, 0.2),
     'L3_conv_b1': (0.0, 0.8),
     'L3_conv_gamma': (1.0, 0.2),
     'L3_conv_beta': (0.0, 0.1)}
    factors = {'L2_conv_b_qk': 7.649}
    for name, (base, spread) in spreads.items():
        noise = np.random.default_rng([zlib.crc32(name.encode()), seed]).standard_normal(out[name].shape)
        drawn = base * np.exp(spread * noise) if base else spread * noise
        out[name] = jnp.asarray(drawn.astype(out[name].dtype))
    for name, factor in factors.items():
        out[name] = (out[name] * factor).astype(out[name].dtype)
    return out
```

```python
import numpy as np
import concourse.bass as bass
from concourse import mybir
from contextlib import ExitStack

P = 128
B, H, W, C = 8, 128, 128, 32
G = P // C
NS = B // G
PIX = W * H
MULTI = 4
HEADS, WS = 4, 8
CK = C // HEADS
NWIN = W // WS
N = WS * WS
TAPS = 4
OW, OH = 5, 13
PW, PH = OW + TAPS - 1, OH + TAPS - 1
STRIPS = -(-W // OW)
PATCHES = -(-H // OH)
HPAD = OH * PATCHES + TAPS - 1
LAST_W = W - OW * (STRIPS - 1)
COLS = 96
K9 = 9
BANK = 512
RING = 2
GN_EPS, BN_EPS, LEAKY = 1e-5, 1e-3, 0.3

FIELDS = [
    ("ident", P), ("wg", MULTI * G * C), ("w2", C), ("fir", COLS), ("wk", P), ("temp", P), ("bk", P),
    ("keep", 2 * P), ("wq", HEADS * N), ("bq", (NWIN // 2) * P), ("w9", COLS), ("b9", G * K9),
    ("shift", 3 * P), ("mean8", P), ("w1", MULTI), ("gamma", 1), ("beta", 1), ("gn_eps", 1), ("bn_eps", 1),
    ("root", 1), ("minus", 1), 
]
AT, _n = {}, 0
for _name, _size in FIELDS:
    AT[_name] = (_n, _size)
    _n += _size
NCONST = _n


def build(nc, x, consts, choose, out):
    fp32 = mybir.dt.float32
    ALU = mybir.AluOpType
    ACT = mybir.ActivationFunctionType
    ds = bass.ds
    ctx = ExitStack()
    with ctx:
        def sb(name, cols):
            return ctx.enter_context(nc.sbuf_tensor(name, [P, cols], fp32))

        def sem(name):
            return ctx.enter_context(nc.semaphore(name))

        X = sb("X", NS * PIX)
        cst = sb("cst", NCONST)
        ST = sb("ST", NS * 4 * H)
        MW = NWIN * NWIN * (C + 1)
        work = sb("work", MW + 7168)
        stats = sb("stats", 64 * 6)
        mv = sb("mv", 2)
        co = sb("co", 16)
        l0s = sb("l0s", 2 * MULTI)
        vall = sb("vall", 4 * NS)
        bns = sb("bns", 16)
        ps = ctx.enter_context(nc.psum_tensor("ps", [P, 8, BANK], fp32))

        X3 = X[:, :].rearrange("p (w h) -> p w h", h=H)
        X5 = X[:, :].rearrange("p (b w h) -> p b w h", w=W // 4, h=H)
        X4 = X[:, :].rearrange("p (j w h) -> p j w h", w=NWIN, h=H)

        def c(name, rows=slice(0, P)):
            a, n = AT[name]
            return cst[rows, a:a + n]

        ident = c("ident")
        wg = c("wg").rearrange("p (j m o) -> p j m o", j=G, m=MULTI)
        wq = c("wq").rearrange("p (h n) -> p h n", h=HEADS)
        bq = c("bq").rearrange("p (q n) -> p q n", q=NWIN // 2)
        shift = c("shift").rearrange("p (k n) -> p k n", k=3)
        rstd, nmr, minus_mean = co[:, 0:1], co[:, 1:2], co[:, 2:3]
        ve = co[:, 3:4]

        def columns(s, w):
            return X5[:, ds(s * 4, 4), ds(w, 1), :].rearrange("p b o h -> p (b o) h")

        def rows4(v):
            return v.rearrange("p (b h) -> p b h", b=4)

        def part(at, shape):
            n = int(np.prod(shape))
            v = work[:, at:at + n]
            names = "abcdef"[:len(shape)]
            pat = "p (" + " ".join(names) + ") -> p " + " ".join(names)
            return v.rearrange(pat, **{k: s for k, s in zip(names[1:], shape[1:])}), at + n

        LOADS, LW = 4, 8
        stage, _e = part(0, [LOADS, G, LW * C])
        lined, _ = part(_e, [RING, LW, G, C])
        yb, _e = part(0, [RING, MULTI, 1024])
        zb, _ = part(_e, [RING, 2, BANK])
        strip, _e = part(0, [RING, HPAD, PW])
        patch, _ = part(_e, [RING, PATCHES, P])
        mall, _e0 = part(0, [NWIN, NWIN, C + 1])
        xn, _e = part(_e0, [RING, NWIN, WS, WS])
        xw, _e = part(_e, [RING, 4, P])
        kh, _e = part(_e, [RING, 4, G, P])
        mh, _e = part(_e0, [RING, NWIN, G, C])
        sums, _ = part(_e, [8, P])
        xs, _ = part(_e0, [NWIN, HEADS, NWIN])
        rs, _e = part(_e, [RING, 4, P])
        sT, _e = part(_e, [NWIN, P])
        T, _e = part(0, [W + 2, G * K9])
        xc, _e = part(_e, [RING, BANK])
        s_rows, _e = part(_e, [W * G])
        sel, _e = part(_e, [W // 4, P])
        vb, _e = part(_e, [RING, BANK])
        assert 4 * RING * BANK + RING * G * 4 * 4 * C + 4096 <= MW + 7168
        ob, _o = part(_e, [RING, G, 4, 4, C])
        yv, _o = part(0, [RING, BANK])
        lv, _o = part(_o, [RING, BANK])
        ov, _o = part(_o, [RING, BANK])
        assert _o <= 5704

        ring_sems = {}

        def rsem(name, owner):
            s = sem(name)
            ring_sems.setdefault(owner, []).append(s)
            return s

        def after(n):
            return n + 1 + RING

        def slot(n):
            return n + 1

        s_const = sem("consts_loaded")
        s_wk = sem("wk_scaled")
        s_stage = sem("stage_ended")
        s_passed = sem("wait_passed")
        s_load = [sem(f"chunk_loaded{u}") for u in range(LOADS)]
        s_lined = sem("chunk_lined_up")
        s_in = sem("bank_transposed")
        s_inst = sem("bank_measured")
        s_bank = sem("bank_copied")
        s_aggr = sem("moments_ready")
        s_pool = sem("pool_step")
        s_y = sem("y_ready")
        s_zp = sem("z_summed")
        s_zs = rsem("z_ready", "act")
        s_w2 = rsem("w2_summed", "pe")
        s_x1 = rsem("x1_written", "dve")
        s_strip = sem("strip_ready")
        s_zero = sem("buffers_zeroed")
        s_pt = sem("patches_transposed")
        s_pc = rsem("patches_copied", "act")
        s_cv = sem("half_filtered")
        s_x2 = rsem("x2_written", "dve")
        s_xn = sem("windows_normalised")
        s_wt = sem("windows_projected")
        s_xw = rsem("xw_ready", "act")
        s_kh = rsem("kh_ready", "dve")
        s_m = rsem("m_summed", "pe")
        s_mc = rsem("m_copied", "act")
        s_sp = sem("sums_projected")
        s_st = sem("sums_step")
        s_mh = sem("mh_ready")
        s_r = sem("r_summed")
        s_rc = rsem("r_copied", "act")
        s_xt = rsem("r_transposed", "pe")
        s_x3 = rsem("x3_written", "dve")
        s_xc = sem("x3n_ready")
        s_tp = rsem("t_projected", "pe")
        s_td = rsem("t_stored", "dve")
        s_sm = sem("s_summed")
        s_ss = sem("s_stored")
        s_sel = sem("sel_loaded")
        s_sc = rsem("s_spread", "pe")
        s_v = rsem("v_ready", "dve")
        s_g = sem("bn_step")
        s_fc = rsem("out_s_spread", "pe")
        s_fv = rsem("out_v_ready", "dve")
        s_fy = rsem("out_y_ready", "act")
        s_fl = rsem("out_l_ready", "dve")
        s_fo = rsem("out_sum_ready", "pool")
        s_ft = rsem("out_transposed", "pe")
        s_fe = rsem("out_chunk_ready", "act")
        s_cur = sem("coefficients_chosen")
        s_out = [sem(f"chunk_stored{u}") for u in range(RING)]

        STAGES = 9
        ENG = 5

        def alone(eng):
            eng.sem_inc(s_passed, 1)

        def stage_end(eng, s, k):
            eng.drain().then_inc(s_stage, 1)
            eng.wait_ge(s_stage, s * (STAGES * ENG) + (k + 1) * ENG)
            alone(eng)

        def start_rings(eng, owner):
            for s in ring_sems.get(owner, []):
                eng.sem_inc(s, RING)

        def spread_s(s, n, bank):
            return nc.tensor.matmul(ps[:, bank, :], sel[:, n, :], ST[:, ds(s * (4 * H), 4 * H)], start=True, stop=True)

        block = ctx.enter_context(nc.Block())

        @block.sync
        def _(sp):
            sp.dma_start(cst[:, :], consts[:, :]).then_inc(s_const, 16)
            with sp.Fori(0, NS) as s:
                def load(n, u):
                    sp.dma_start(stage[:, u, :, :],
                                 x[ds(s * G, G), :, ds(n * LW, LW), :].rearrange("g h w c -> h g (w c)")
                                 ).then_inc(s_load[u], 16)
                for u in range(LOADS):
                    load(u, u)
                with sp.Fori(1, W // LW // LOADS) as i:
                    for u in range(LOADS):
                        sp.wait_ge(s_lined, s * 16 + i * 4 + (u - 3))
                        alone(sp)
                        load(i * LOADS + u, u)
                for k in range(STAGES):
                    if k == 5:
                        sp.dma_start(sel[:, :, :], choose[:, :, :]).then_inc(s_sel, 16)
                    stage_end(sp, s, k)
            with sp.Fori(0, NS) as s:
                with sp.Fori(0, 4) as i:
                    for u in range(RING):
                        sp.wait_ge(s_fe, after(s * 32 + i * 8 + (4 * u + 3)))
                        for g in range(G):
                            o = out.rearrange("i h (b w) c -> h i b (w c)", b=4)
                            o = o[:, ds(s * G + g, 1), :, ds(i * (8 * C) + 4 * C * u, 4 * C)].rearrange("h a b w -> h (a b) w")
                            sp.dma_start(o, ob[:, u, g, :, :, :].rearrange("p b w c -> p b (w c)")).then_inc(s_out[u], 16)
            for u in range(RING):
                sp.wait_ge(s_out[u], NS * 4 * 64 + 64)

        @block.tensor
        def _(pe):
            start_rings(pe, "pe")
            pe.sem_inc(s_in, 2 * RING)
            pe.sem_inc(s_cv, 2 * RING)
            pe.sem_inc(s_r, 2 * RING)
            pe.wait_ge(s_const, 16)
            with pe.Fori(0, NS) as s:
                with pe.Fori(0, W // LW // LOADS) as i:
                    for u in range(LOADS):
                        pe.wait_ge(s_lined, s * 16 + i * 4 + (u + 1))
                        for b in range(2):
                            pe.wait_ge(s_bank, s * 32 + i * 8 + (2 * u + b + 1))
                            for w in range(4):
                                last = pe.transpose(ps[:, 2 * u + b, w * H:(w + 1) * H],
                                                    lined[:, u % 2, 4 * b + w, :, :].rearrange("p g c -> p (g c)"), ident)
                            last.then_inc(s_in, 1)
                stage_end(pe, s, 0)

                def wg_sum(i, q):
                    jp, hh, un = q % 2, (q // 2) % 2, q // 4
                    if q % 4 == 0:
                        pe.wait_ge(s_y, s * 16 + i * 2 + (un + 1))
                    pe.wait_ge(s_zs, slot(s * 64 + i * 8 + q))
                    for jj in range(2):
                        for m in range(MULTI):
                            last = pe.matmul(ps[C * m:C * m + C, 2 * (q % 2) + jj, :], wg[:, 2 * jp + jj, m, :],
                                             yb[:, un, m, BANK * hh:BANK * hh + BANK], start=True, stop=True)
                    last.then_inc(s_zp, 1)

                def w2_sum(i, q):
                    jp, hh = q % 2, (q // 2) % 2
                    pe.wait_ge(s_zs, after(s * 64 + i * 8 + q))
                    if jp == 0:
                        pe.wait_ge(s_x1, slot(s * 32 + i * 4 + q // 2))
                    for jj in range(2):
                        j = 2 * jp + jj
                        last = pe.matmul(ps[C * j:C * j + C, 4 + hh, :], c("w2"), zb[:, q % 2, jj, :],
                                         start=True, stop=True)
                    last.then_inc(s_w2, 1)

                for q in range(8):
                    wg_sum(0, q)
                    if q:
                        w2_sum(0, q - 1)
                with pe.Fori(1, 8) as i:
                    for q in range(8):
                        wg_sum(i, q)
                        w2_sum(i, q - 1)
                w2_sum(7, 7)
                stage_end(pe, s, 1)

                def to_patches(t, u):
                    pe.wait_ge(s_strip, s * STRIPS + t + 1)
                    pe.wait_ge(s_pc, slot(s * STRIPS + t))
                    for k in range(PATCHES):
                        at = 3 * BANK * u + k * P
                        last = pe.transpose(ps[:, at // BANK, at % BANK:at % BANK + P],
                                            strip[:, u, OH * k:OH * k + PH, :].rearrange("p h w -> p (h w)"), ident)
                    last.then_inc(s_pt, 1)

                def filtered(t, u):
                    pe.wait_ge(s_pc, after(s * STRIPS + t))
                    for hf in range(2):
                        pe.wait_ge(s_x2, slot(s * (2 * STRIPS) + t * 2 + hf))
                        for k in range(PATCHES // 2):
                            last = pe.matmul(ps[:, 6 + hf, COLS * k:COLS * k + COLS],
                                             patch[:, u, hf * (PATCHES // 2) + k, :], c("fir"), start=True, stop=True)
                        last.then_inc(s_cv, 1)

                to_patches(0, 0)
                with pe.Fori(0, STRIPS // 2 - 1) as i:
                    for u in range(2):
                        to_patches(i * 2 + (u + 1), 1 - u)
                        filtered(i * 2 + u, u)
                to_patches(STRIPS - 1, 1)
                filtered(STRIPS - 2, 0)
                filtered(STRIPS - 1, 1)
                stage_end(pe, s, 2)

                def project(w1, n, xu, hf):
                    nn = s * 32 + n
                    if hf == 0:
                        pe.wait_ge(s_xn, s * 16 + w1 + 1)
                    pe.wait_ge(s_xw, slot(nn))
                    pe.wait_ge(s_kh, slot(nn))
                    for what, bank in ((ident, 0), (c("wk"), 2)):
                        for pp in range(4):
                            h1 = 2 * (4 * hf + pp)
                            px = xn[:, xu, h1:h1 + 2, :, :].rearrange("p h j i -> p (h j i)")
                            o = ps[:, bank + hf, pp * P:pp * P + P]
                            if bank == 0:
                                pe.transpose(o, px, what)
                            else:
                                last = pe.matmul(o, px, what, start=True, stop=True)
                    last.then_inc(s_wt, 1)

                def m_sum(n, u):
                    nn = s * 32 + n
                    pe.wait_ge(s_xw, after(nn))
                    pe.wait_ge(s_kh, after(nn))
                    pe.wait_ge(s_mc, slot(nn))
                    for pp in range(4):
                        for g in range(G):
                            last = pe.matmul(ps[C * g:C * g + C, 4 + u, pp * P:pp * P + P],
                                             xw[:, u, pp, C * g:C * g + C], kh[:, u, pp, g, :],
                                             start=True, stop=True)
                    last.then_inc(s_m, 1)

                project(0, 0, 0, 0)
                project(0, 1, 0, 1)
                m_sum(0, 0)
                with pe.Fori(0, 7) as i:
                    for u in range(2):
                        w1 = i * 2 + (u + 1)
                        project(w1, w1 * 2, 1 - u, 0)
                        m_sum(w1 * 2 - 1, 1)
                        project(w1, w1 * 2 + 1, 1 - u, 1)
                        m_sum(w1 * 2, 0)
                project(15, 30, 1, 0)
                m_sum(29, 1)
                project(15, 31, 1, 1)
                m_sum(30, 0)
                m_sum(31, 1)
                pe.wait_ge(s_st, s * 2 + 1)
                for pr in range(NWIN // 2):
                    v = xs[:, 2 * pr:2 * pr + 2, :, :].rearrange("p a b c -> p (a b c)")
                    last = pe.matmul(ps[:, 6 + pr // 4, (pr % 4) * P:(pr % 4) * P + P], v, c("wk"), start=True, stop=True)
                last.then_inc(s_sp, 1)
                stage_end(pe, s, 3)

                def r_sum(w1, n, mu, hf):
                    nn = s * 32 + n
                    if hf == 0:
                        pe.wait_ge(s_mh, s * 16 + w1 + 1)
                    pe.wait_ge(s_rc, slot(nn))
                    for q in range(4):
                        pe.matmul(ps[:, hf, q * P:q * P + P], bq[:, 4 * hf + q, :],
                                  sT[:, ds(w1, 1), :].rearrange("p a b -> p (a b)"), start=(q == 0), stop=False)
                    for hp in range(2):
                        for hd in range(HEADS):
                            mvg = mh[:, mu, 8 * hf + hp:8 * hf + hp + 7:2, :, hd * CK:hd * CK + CK]
                            o = ps[N * hp:N * hp + N, hf, :].rearrange("p (q g d) -> p q g d", q=4, g=G)
                            last = pe.matmul(o[:, :, :, hd * CK:hd * CK + CK], wq[:, hd, :], mvg,
                                             start=False, stop=(hd == HEADS - 1))
                    last.then_inc(s_r, 1)

                def r_back(n, u):
                    nn = s * 32 + n
                    pe.wait_ge(s_rc, after(nn))
                    pe.wait_ge(s_x3, slot(nn))
                    for q in range(4):
                        last = pe.transpose(ps[:, 2 + u, q * P:q * P + P], rs[:, u, q, :], ident)
                    last.then_inc(s_xt, 1)

                r_sum(0, 0, 0, 0)
                r_sum(0, 1, 0, 1)
                r_back(0, 0)
                with pe.Fori(0, 7) as i:
                    for u in range(2):
                        w1 = i * 2 + (u + 1)
                        r_sum(w1, w1 * 2, 1 - u, 0)
                        r_back(w1 * 2 - 1, 1)
                        r_sum(w1, w1 * 2 + 1, 1 - u, 1)
                        r_back(w1 * 2, 0)
                r_sum(15, 30, 1, 0)
                r_back(29, 1)
                r_sum(15, 31, 1, 1)
                r_back(30, 0)
                r_back(31, 1)
                stage_end(pe, s, 4)

                with pe.Fori(0, 16) as i:
                    for u in range(2):
                        nn = s * 32 + i * 2 + u
                        pe.wait_ge(s_xc, nn + 1)
                        pe.wait_ge(s_td, slot(nn))
                        for w in range(4):
                            last = pe.matmul(ps[:, u, w * COLS:w * COLS + COLS], xc[:, u, w * H:w * H + H], c("w9"),
                                             start=True, stop=True)
                        last.then_inc(s_tp, 1)
                stage_end(pe, s, 5)
                for k in range(K9):
                    ki, kj = divmod(k, 3)
                    mvg = T[:, 2 - kj:2 - kj + W, :].rearrange("p w (g k) -> p w g k", k=K9)[:, :, :, k]
                    last = pe.matmul(ps[:, 7, :], shift[:, ki, :], mvg, start=(k == 0), stop=(k == K9 - 1))
                last.then_inc(s_sm, 1)
                pe.wait_ge(s_ss, s + 1)
                for b in range(4):
                    last = pe.transpose(ps[:, 6, b * H:b * H + H], s_rows[:, b * P:b * P + P], ident)
                last.then_inc(s_sm, 1)
                stage_end(pe, s, 6)
                pe.wait_ge(s_sel, s * 16 + 16)
                for n in range(32):
                    pe.wait_ge(s_v, slot(s * 32 + n))
                    spread_s(s, n, n % 2).then_inc(s_sc, 1)
                stage_end(pe, s, 7)
                stage_end(pe, s, 8)
            pe.wait_ge(s_g, 2)
            pe.matmul(ps[:, 0, 0:NS], c("mean8"), bns[:, 0:2], start=True, stop=True).then_inc(s_g, 1)
            pe.wait_ge(s_g, 7)
            pe.matmul(ps[:, 1, 0:NS], c("mean8"), bns[:, 4:6], start=True, stop=True).then_inc(s_g, 1)
            with pe.Fori(0, NS) as s:
                def out_t(n, u):
                    nn = s * 32 + n
                    pe.wait_ge(s_fo, after(nn))
                    pe.wait_ge(s_fe, slot(nn))
                    for w in range(4):
                        last = pe.transpose(ps[:, 4 + u, w * P:w * P + P], ov[:, u, w * H:w * H + H], ident)
                    last.then_inc(s_ft, 1)

                def out_s(n, u):
                    nn = s * 32 + n
                    pe.wait_ge(s_fv, slot(nn))
                    spread_s(s, n, 2 + u).then_inc(s_fc, 1)

                out_s(0, 0)
                for n in range(31):
                    out_s(n + 1, 1 - n % 2)
                    out_t(n, n % 2)
                out_t(31, 1)

        @block.scalar
        def _(act):
            start_rings(act, "act")
            act.sem_inc(s_bank, 8)
            act.sem_inc(s_out[0], 64)
            act.sem_inc(s_out[1], 64)
            with act.Fori(0, NS) as s:
                with act.Fori(0, 4) as i:
                    for b in range(8):
                        act.wait_ge(s_inst, s * 32 + i * 8 + b + 1)
                        act.activation(X[:, ds(s * PIX + i * 8 * BANK + b * BANK, BANK)], ps[:, b, :], ACT.Copy
                                       ).then_inc(s_bank, 1)
                stage_end(act, s, 0)

                def gelu_y(n, u, m):
                    o = act.activation(yb[:, u, m, :], X[:, ds(s * PIX + n * 1024, 1024)], ACT.Gelu,
                                       scale=l0s[:, m:m + 1], bias=l0s[:, MULTI + m:MULTI + m + 1])
                    if m == MULTI - 1:
                        o.then_inc(s_y, 1)

                def gelu_z(i, q):
                    nn = s * 64 + i * 8 + q
                    act.wait_ge(s_zp, nn + 1)
                    act.wait_ge(s_w2, slot(nn))
                    act.activation(zb[:, q % 2, :, :].rearrange("p a b -> p (a b)"),
                                   ps[:, 2 * (q % 2):2 * (q % 2) + 2, :].rearrange("p a b -> p (a b)"),
                                   ACT.Gelu).then_inc(s_zs, 1)

                def gates(i, last=False):
                    for un in range(2):
                        nxt = not (last and un == 1)
                        for pc in range(4):
                            gelu_z(i, 4 * un + pc)
                            if nxt:
                                for m in ((0, 1), (2,), (3,), ())[pc]:
                                    gelu_y(i * 2 + (un + 1), 1 - un, m)

                for m in range(MULTI):
                    gelu_y(0, 0, m)
                with act.Fori(0, 7) as i:
                    gates(i)
                gates(7, last=True)
                stage_end(act, s, 1)

                with act.Fori(0, STRIPS // 2) as i:
                    for u in range(2):
                        nn = s * STRIPS + i * 2 + u
                        act.wait_ge(s_pt, nn + 1)
                        act.wait_ge(s_cv, nn * 2 + 2)
                        act.activation(patch[:, u, :, :].rearrange("p a b -> p (a b)"),
                                       ps[:, 3 * u:3 * u + 3, :].rearrange("p a b -> p (a b)")[:, 0:PATCHES * P],
                                       ACT.Copy).then_inc(s_pc, 1)
                stage_end(act, s, 2)

                def copy_xw(n, u):
                    nn = s * 32 + n
                    act.wait_ge(s_wt, nn + 1)
                    act.wait_ge(s_m, slot(nn))
                    act.activation(xw[:, u, :, :].rearrange("p a b -> p (a b)"), ps[:, u, :], ACT.Copy
                                   ).then_inc(s_xw, 1)

                def copy_m(n, u):
                    nn = s * 32 + n
                    act.wait_ge(s_m, after(nn))
                    src = ps[:, 4 + u, :].rearrange("p (a b) -> p a b", b=N)[:, :, 0:C + 1]
                    dst = work[:, ds(n * (8 * (C + 1)), 8 * (C + 1))].rearrange("p (a b) -> p a b", b=C + 1)
                    act.activation(dst, src, ACT.Copy).then_inc(s_mc, 1)

                copy_xw(0, 0)
                with act.Fori(0, 15) as i:
                    for u in range(2):
                        copy_xw(i * 2 + (u + 1), 1 - u)
                        copy_m(i * 2 + u, u)
                copy_xw(31, 1)
                copy_m(30, 0)
                copy_m(31, 1)
                stage_end(act, s, 3)

                def spread_m(w1, u):
                    act.wait_ge(s_r, s * 32 + w1 * 2 + 2)
                    for g in range(G):
                        src = work[C * g:C * g + C, ds(w1 * (NWIN * (C + 1)), NWIN * (C + 1))
                                   ].rearrange("p (a b) -> p a b", b=C + 1)[:, :, 0:C]
                        last = act.activation(mh[C * g:C * g + C, u, :, g, :], src, ACT.Copy)
                    last.then_inc(s_mh, 1)

                def copy_r(n, u):
                    nn = s * 32 + n
                    act.wait_ge(s_r, after(nn) + RING)
                    act.wait_ge(s_xt, slot(nn))
                    act.activation(rs[:, u, :, :].rearrange("p a b -> p (a b)"), ps[:, u, :], ACT.Copy
                                   ).then_inc(s_rc, 1)

                act.wait_ge(s_zero, s * 3 + 3)
                spread_m(0, 0)
                with act.Fori(0, 7) as i:
                    for u in range(2):
                        w1 = i * 2 + u
                        spread_m(w1 + 1, 1 - u)
                        copy_r(w1 * 2, 0)
                        copy_r(w1 * 2 + 1, 1)
                spread_m(15, 1)
                for n in range(28, 32):
                    copy_r(n, n % 2)
                stage_end(act, s, 4)

                with act.Fori(0, 16) as i:
                    for u in range(2):
                        nn = s * 32 + i * 2 + u
                        act.wait_ge(s_tp, slot(nn))
                        act.activation(xc[:, u, :], X[:, ds(s * PIX + i * 2 * BANK + u * BANK, BANK)], ACT.Identity,
                                       scale=rstd, bias=nmr).then_inc(s_xc, 1)
                for k in range(5, STAGES):
                    stage_end(act, s, k)
            with act.Fori(0, NS) as s:
                def norm(n, u):
                    nn = s * 32 + n
                    act.wait_ge(s_fv, after(nn))
                    act.wait_ge(s_fl, slot(nn))
                    act.activation(yv[:, u, :], vb[:, u, :], ACT.Identity, scale=co[:, 8:9], bias=co[:, 9:10]
                                   ).then_inc(s_fy, 1)

                def lay(n, j, k, i):
                    act.wait_ge(s_ft, after(s * 32 + n))
                    if j == 0:
                        act.wait_ge(s_out[k], s * 256 + i * 64 + 64)
                    o = ob[:, k, :, :, j, :].rearrange("p g b c -> p b g c")
                    act.activation(o, ps[:, 4 + j % 2, :].rearrange("p (b g c) -> p b g c", b=4, g=G), ACT.Copy
                                   ).then_inc(s_fe, 1)

                norm(0, 0)
                with act.Fori(0, 3) as i:
                    for j in range(8):
                        norm(i * 8 + (j + 1), (j + 1) % 2)
                        lay(i * 8 + j, j % 4, j // 4, i)
                for j in range(8):
                    if j < 7:
                        norm(25 + j, (j + 1) % 2)
                    lay(24 + j, j % 4, j // 4, 3)

        @block.vector
        def _(dve):
            start_rings(dve, "dve")
            dve.wait_ge(s_const, 16)
            dve.tensor_tensor(c("wk"), c("wk"), c("temp"), ALU.mult)
            dve.tensor_tensor(c("bk"), c("bk"), c("temp"), ALU.mult).then_inc(s_wk, 1)
            dve.wait_ge(s_wk, 1)
            with dve.Fori(0, NS) as s:
                def measure(i, u):
                    for b in range(2 * u, 2 * u + 2):
                        dve.wait_ge(s_in, after(s * 32 + i * 8 + b) + RING)
                        dve.bn_stats(stats[:, ds(i * 48 + 6 * b, 6)], ps[:, b, :]).then_inc(s_inst, 1)

                def moments(n):
                    dve.drain()
                    dve.bn_aggr(mv[:, :], stats[:, 0:6 * n]).then_inc(s_aggr, 1)

                with dve.Fori(0, 4) as i:
                    for u in range(LOADS):
                        dve.wait_ge(s_load[u], s * 64 + i * 16 + 16)
                        dve.wait_ge(s_in, s * 32 + i * 8 + (2 * u + 2))
                        dve.tensor_copy(lined[:, u % 2, :, :, :],
                                        stage[:, u, :, :].rearrange("p g (w c) -> p w g c", c=C)).then_inc(s_lined, 1)
                        if u:
                            measure(i, u - 1)
                    measure(i, LOADS - 1)
                moments(32)
                stage_end(dve, s, 0)

                with dve.Fori(0, 16) as i:
                    for u in range(2):
                        nn = s * 32 + i * 2 + u
                        dve.wait_ge(s_w2, after(nn * 2 + 1))
                        v = X[:, ds(s * PIX + i * 2 * BANK + u * BANK, BANK)]
                        dve.tensor_tensor(v, v, ps[:, 4 + u, :], ALU.add).then_inc(s_x1, 1)
                        dve.wait_ge(s_x1, after(nn))
                        alone(dve)
                        dve.bn_stats(stats[:, ds(i * 12 + 6 * u, 6)], v)
                moments(32)
                stage_end(dve, s, 1)

                def norm_strip(t, u, lo, hi):
                    o = strip[:, u, 1:1 + H, lo:hi].rearrange("p h w -> p w h")
                    dve.tensor_scalar(o, X3[:, ds(s * W + t * OW + (lo - 1), hi - lo), :], rstd, nmr,
                                      ALU.mult, ALU.add).then_inc(s_strip, 1)

                half = OH * PATCHES // 2

                def add_filtered(t, u, ow):
                    nn = s * (2 * STRIPS) + t * 2
                    w0 = s * W + t * OW
                    for hf in range(2):
                        dve.wait_ge(s_cv, after(nn + hf) + RING)
                        rows = ((0, 5),) if hf == 0 else ((0, 4), (4, 5))
                        for k0, k1 in rows:
                            h0 = hf * half + k0 * OH
                            nk, nh = k1 - k0, min(OH, H - h0)
                            src = ps[:, 6 + hf, 0:5 * COLS].rearrange("p (k n) -> p k n", n=COLS)[:, k0:k1, 0:ow * OH]
                            src = src.rearrange("p k (w h) -> p w k h", h=OH)[:, :, :, 0:nh]
                            v = X3[:, ds(w0, ow), h0:h0 + nk * nh].rearrange("p w (k h) -> p w k h", h=nh)
                            last = dve.tensor_tensor(v, v, src, ALU.add)
                        last.then_inc(s_x2, 1)
                    dve.wait_ge(s_x2, after(nn + 1))
                    alone(dve)
                    for hf, (a, b) in enumerate(((0, half), (half, H))):
                        dve.bn_stats(stats[:, ds(t * 12 + 6 * hf, 6)], X3[:, ds(w0, ow), a:b])

                dve.wait_ge(s_zero, s * 3 + 1)
                norm_strip(0, 0, 1, PW)
                norm_strip(1, 1, 0, PW)
                with dve.Fori(0, STRIPS // 2 - 2) as i:
                    for u in range(2):
                        add_filtered(i * 2 + u, u, OW)
                        norm_strip(i * 2 + (u + 2), u, 0, PW)
                add_filtered(STRIPS - 4, 0, OW)
                norm_strip(STRIPS - 2, 0, 0, PW)
                add_filtered(STRIPS - 3, 1, OW)
                dve.memset(strip[:, 1, 1:1 + H, LAST_W + 1:PW], 0.0)
                norm_strip(STRIPS - 1, 1, 0, LAST_W + 1)
                add_filtered(STRIPS - 2, 0, OW)
                add_filtered(STRIPS - 1, 1, LAST_W)
                moments(2 * STRIPS)
                stage_end(dve, s, 2)

                def norm_windows(w1, u):
                    dve.tensor_scalar(xn[:, u, :, :, :].rearrange("p h j i -> p j i h"),
                                      X4[:, ds(s * 8, 8), ds(w1, 1), :].rearrange("p j a (i h) -> p (j a) i h", i=WS),
                                      rstd, nmr, ALU.mult, ALU.add).then_inc(s_xn, 1)

                def keys(n, u):
                    nn = s * 32 + n
                    dve.wait_ge(s_wt, nn + 1)
                    dve.wait_ge(s_m, slot(nn))
                    for hp in range(2):
                        rows = slice(N * hp, N * hp + N)
                        k_in = ps[rows, 2 + u, :].rearrange("p (a g d) -> p a g d", a=4, g=G)
                        bias = c("bk", rows).rearrange("p (o g d) -> p o g d", o=1, g=G).broadcast_to([N, 4, G, C])
                        o = kh[rows, u, :, :, N * hp:N * hp + C]
                        last = dve.tensor_tensor(o, k_in, bias, ALU.add)
                    last.then_inc(s_kh, 1)

                dve.wait_ge(s_zero, s * 3 + 2)
                norm_windows(0, 0)
                norm_windows(1, 1)
                with dve.Fori(0, 7) as i:
                    for u in range(2):
                        w1 = i * 2 + u
                        keys(w1 * 2, 0)
                        keys(w1 * 2 + 1, 1)
                        norm_windows(w1 + 2, u)
                for n in range(28, 32):
                    keys(n, n % 2)
                dve.wait_ge(s_mc, after(s * 32 + 31))
                dve.tensor_copy(xs[:, :, :, :], mall[:, :, :, C:C + 1].rearrange("p a b o -> p a o b"
                                                                                ).broadcast_to([P, NWIN, HEADS, NWIN])
                                ).then_inc(s_st, 1)
                dve.wait_ge(s_sp, s + 1)
                dve.scalar_tensor_tensor(
                    sums, c("bk").rearrange("p (o n) -> p o n", o=1).broadcast_to([P, 8, P]), float(N),
                    ps[:, 6:8, :].rearrange("p a (b n) -> p (a b) n", n=P), ALU.mult, ALU.add).then_inc(s_st, 1)
                dve.wait_ge(s_st, s * 2 + 2)
                for par in range(2):
                    keep = c("keep")[:, par * P:par * P + P].rearrange("p (o n) -> p o n", o=1).broadcast_to([P, 8, P])
                    dve.tensor_tensor(sT[:, par:NWIN:2, :], sums, keep, ALU.mult)
                stage_end(dve, s, 3)

                with dve.Fori(0, 16) as i:
                    for hf in range(2):
                        nn = s * 32 + i * 2 + hf
                        dve.wait_ge(s_xt, after(nn))
                        v = X3[:, ds(s * W + i * WS, WS), 64 * hf:64 * hf + 64]
                        src = ps[:, 2 + hf, :].rearrange("p (q j i) -> p j q i", j=WS, i=WS)
                        v4 = v.rearrange("p j (q i) -> p j q i", i=WS)
                        dve.tensor_tensor(v4, v4, src, ALU.add).then_inc(s_x3, 1)
                        dve.wait_ge(s_x3, after(nn))
                        alone(dve)
                        dve.bn_stats(stats[:, ds(i * 12 + 6 * hf, 6)], v)
                moments(32)
                stage_end(dve, s, 4)

                with dve.Fori(0, 16) as i:
                    for u in range(2):
                        nn = s * 32 + i * 2 + u
                        dve.wait_ge(s_tp, after(nn))
                        o = T[:, ds(i * 8 + 4 * u + 1, 4), :]
                        bias = c("b9").rearrange("p (o n) -> p o n", o=1).broadcast_to([P, 4, G * K9])
                        src = ps[:, u, 0:4 * COLS].rearrange("p (w n) -> p w n", n=COLS)[:, :, 0:G * K9]
                        dve.tensor_tensor(o, src, bias, ALU.add).then_inc(s_td, 1)
                dve.drain()
                dve.memset(T[:, 0:2, :], 0.0)
                dve.memset(T[:, W:W + 2, :], 0.0)
                stage_end(dve, s, 5)
                dve.wait_ge(s_sm, s * 2 + 1)
                dve.tensor_copy(s_rows[:, :], ps[:, 7, :]).then_inc(s_ss, 1)
                dve.wait_ge(s_sm, s * 2 + 2)
                dve.tensor_copy(ST[:, ds(s * (4 * H), 4 * H)], ps[:, 6, :])
                stage_end(dve, s, 6)
                with dve.Fori(0, 16) as i:
                    for u in range(2):
                        nn = s * 32 + i * 2 + u
                        dve.wait_ge(s_sc, after(nn))
                        dve.scalar_tensor_tensor(rows4(vb[:, u, :]), columns(s, i * 2 + u), minus_mean, rows4(ps[:, u, :]),
                                                 ALU.add, ALU.mult).then_inc(s_v, 1)
                        dve.wait_ge(s_v, after(nn))
                        alone(dve)
                        dve.bn_stats(stats[:, ds(i * 12 + 6 * u, 6)], vb[:, u, :])
                moments(32)
                stage_end(dve, s, 7)
                dve.tensor_copy(vall[:, ds(s * 4, 2)], mv[:, :])
                dve.tensor_copy(vall[:, ds(s * 4 + 2, 1)], rstd)
                dve.tensor_copy(vall[:, ds(s * 4 + 3, 1)], minus_mean)
                stage_end(dve, s, 8)
            dve.wait_ge(s_g, 3)
            va = vall[:, :].rearrange("p (s k) -> p k s", k=4)
            steps = [3]

            def step(ins):
                ins.then_inc(s_g, 1)
                steps[0] += 1
                dve.wait_ge(s_g, steps[0])

            step(dve.tensor_reduce(bns[:, 8:9], ps[:, 0, 0:NS], mybir.AxisListType.X, ALU.add))
            step(dve.tensor_scalar(bns[:, 4:6], bns[:, 0:2], bns[:, 8:9], None, ALU.subtract))
            step(dve.tensor_tensor(bns[:, 4:6], bns[:, 4:6], bns[:, 4:6], ALU.mult))
            dve.tensor_tensor(bns[:, 4:6], bns[:, 4:6], bns[:, 2:4], ALU.add).then_inc(s_g, 1)
            dve.wait_ge(s_g, 8)
            steps[0] = 8
            step(dve.tensor_reduce(bns[:, 9:10], ps[:, 1, 0:NS], mybir.AxisListType.X, ALU.add))
            dve.wait_ge(s_g, 11)
            steps[0] = 11
            step(dve.tensor_tensor(bns[:, 11:12], bns[:, 10:11], c("gamma"), ALU.mult))
            step(dve.tensor_tensor(bns[:, 12:14], va[:, 2, :], bns[:, 11:12].broadcast_to([P, 2]), ALU.mult))
            step(dve.tensor_tensor(bns[:, 14:15], bns[:, 8:9], bns[:, 11:12], ALU.mult))
            step(dve.tensor_tensor(bns[:, 15:16], c("beta"), bns[:, 14:15], ALU.subtract))
            with dve.Fori(0, NS) as s:
                dve.wait_ge(s_fy, s * 32 + RING)
                dve.tensor_copy(co[:, 8:9], bns[:, ds(s + 12, 1)])
                dve.tensor_copy(co[:, 9:10], bns[:, 15:16])
                dve.tensor_copy(co[:, 10:11], vall[:, ds(s * 4 + 3, 1)]).then_inc(s_cur, 1)
                dve.wait_ge(s_cur, s + 1)

                def scaled(n, u):
                    nn = s * 32 + n
                    dve.wait_ge(s_fc, after(nn))
                    dve.wait_ge(s_fy, slot(nn))
                    dve.scalar_tensor_tensor(rows4(vb[:, u, :]), columns(s, n), co[:, 10:11], rows4(ps[:, 2 + u, :]),
                                             ALU.add, ALU.mult).then_inc(s_fv, 1)

                def leaky(n, u):
                    nn = s * 32 + n
                    dve.wait_ge(s_fy, after(nn))
                    dve.wait_ge(s_fo, slot(nn))
                    dve.scalar_tensor_tensor(lv[:, u, :], yv[:, u, :], LEAKY, yv[:, u, :], ALU.mult, ALU.max
                                             ).then_inc(s_fl, 1)

                scaled(0, 0)
                with dve.Fori(0, 15) as i:
                    for u in range(2):
                        scaled(i * 2 + (u + 1), 1 - u)
                        leaky(i * 2 + u, u)
                scaled(31, 1)
                leaky(30, 0)
                leaky(31, 1)

        @block.gpsimd
        def _(pool):
            start_rings(pool, "pool")
            pool.wait_ge(s_const, 16)
            PS = 18

            with pool.Fori(0, NS) as s:
                cnt = [0]

                def step(ins):
                    cnt[0] += 1
                    ins.then_inc(s_pool, 1)
                    pool.wait_ge(s_pool, s * PS + cnt[0])
                    alone(pool)

                def coefficients(k):
                    pool.wait_ge(s_aggr, s * 5 + k + 1)
                    step(pool.tensor_tensor(ve, mv[:, 1:2], c("gn_eps"), ALU.add))
                    step(pool.tensor_tensor(rstd, ve, c("root"), ALU.pow))
                    step(pool.tensor_tensor(minus_mean, mv[:, 0:1], c("minus"), ALU.mult))
                    step(pool.tensor_tensor(nmr, minus_mean, rstd, ALU.mult))

                coefficients(0)
                step(pool.tensor_tensor(l0s[:, 0:MULTI], c("w1"), rstd.broadcast_to([P, MULTI]), ALU.mult))
                step(pool.tensor_tensor(l0s[:, MULTI:2 * MULTI], c("w1"), nmr.broadcast_to([P, MULTI]), ALU.mult))
                stage_end(pool, s, 0)
                coefficients(1)
                stage_end(pool, s, 1)
                pool.memset(strip[:, :, :, :], 0.0).then_inc(s_zero, 1)
                coefficients(2)
                stage_end(pool, s, 2)
                pool.memset(kh[:, :, :, :, :], 0.0)
                pool.drain()
                for hp in range(2):
                    last = pool.memset(kh[N * hp:N * hp + N, :, :, :, N * hp + C:N * hp + C + 1], 1.0)
                last.then_inc(s_zero, 1)
                stage_end(pool, s, 3)
                pool.memset(mh[:, :, :, :, :], 0.0).then_inc(s_zero, 1)
                coefficients(3)
                assert cnt[0] == PS
                stage_end(pool, s, 4)
                stage_end(pool, s, 5)
                stage_end(pool, s, 6)
                stage_end(pool, s, 7)
                stage_end(pool, s, 8)
            va = vall[:, :].rearrange("p (s k) -> p k s", k=4)
            pool.tensor_tensor(bns[:, 0:2], va[:, 0, :], va[:, 2, :], ALU.mult).then_inc(s_g, 1)
            pool.tensor_tensor(bns[:, 2:4], va[:, 1, :], va[:, 2, :], ALU.mult)
            pool.drain()
            pool.tensor_tensor(bns[:, 2:4], bns[:, 2:4], va[:, 2, :], ALU.mult).then_inc(s_g, 1)
            pool.wait_ge(s_g, 9)
            pool.tensor_tensor(bns[:, 10:11], bns[:, 9:10], c("bn_eps"), ALU.add).then_inc(s_g, 1)
            pool.wait_ge(s_g, 10)
            pool.tensor_tensor(bns[:, 10:11], bns[:, 10:11], c("root"), ALU.pow).then_inc(s_g, 1)
            with pool.Fori(0, NS) as s:
                def total(n, u):
                    nn = s * 32 + n
                    pool.wait_ge(s_fl, after(nn))
                    pool.wait_ge(s_ft, slot(nn))
                    pool.tensor_tensor(rows4(ov[:, u, :]), columns(s, n), rows4(lv[:, u, :]), ALU.add
                                       ).then_inc(s_fo, 1)

                with pool.Fori(0, 16) as i:
                    for u in range(2):
                        total(i * 2 + u, u)


def constants(w1, wg, w2, fir, W_qk, b_qk, temperature, W9, b9, gamma, beta):
    t = np.zeros((P, NCONST), np.float32)

    def put(name, a):
        at, n = AT[name]
        t[:, at:at + n] = np.asarray(a, np.float32).reshape(P, n)

    put("ident", np.eye(P))
    a = np.zeros((G, C, G, MULTI, C), np.float32)
    for j in range(G):
        a[j, :, j] = wg.transpose(2, 0, 1)
    put("wg", a)
    a = np.zeros((MULTI, C, C), np.float32)
    for m in range(MULTI):
        a[m, range(C), range(C)] = w2[:, m]
    put("w2", a)
    a = np.zeros((PH, PW, COLS), np.float32)
    for w in range(OW):
        for h in range(OH):
            a[h:h + TAPS, w:w + TAPS, w * OH + h] = fir
    put("fir", a)
    a = np.zeros((G, C, G, C), np.float32)
    for g in range(G):
        a[g, :, g] = W_qk[N * HEADS:].T
    put("wk", a)
    heads = np.repeat(temperature, CK)
    put("temp", np.broadcast_to(np.tile(heads, G), (P, P)))
    put("bk", np.broadcast_to(np.tile(b_qk[N * HEADS:], G), (P, P)))
    a = np.zeros((2, HEADS, NWIN, 2, G, HEADS, CK), np.float32)
    for par in range(2):
        for hd in range(HEADS):
            a[par, hd, :, par, :, hd] = 1
    put("keep", a)
    q = W_qk[:N * HEADS].reshape(HEADS, WS, WS, C).transpose(3, 0, 2, 1)
    put("wq", np.broadcast_to(q[None], (G, C, HEADS, WS, WS)))
    bq = b_qk[:N * HEADS].reshape(HEADS, WS, WS).transpose(0, 2, 1).reshape(HEADS, N)
    a = np.zeros((2, HEADS, NWIN, NWIN // 2, 2, N), np.float32)
    for h1 in range(NWIN):
        a[:, :, h1, h1 // 2, h1 % 2] = bq
    put("bq", a)
    a = np.zeros((G, C, COLS), np.float32)
    for g in range(G):
        a[g, :, g * K9:(g + 1) * K9] = W9
    put("w9", a)
    put("b9", np.broadcast_to(np.tile(b9, G), (P, G * K9)))
    a = np.zeros((P, 3, P), np.float32)
    for k in range(3):
        for h in range(1, H - 1):
            a[h, k, h + k - 1] = 1
    put("shift", a)
    put("mean8", np.tile(np.eye(C), (G, G)) / B)
    put("w1", np.tile(w1, (G, 1)))
    put("gamma", np.tile(gamma, G))
    put("beta", np.tile(beta, G))
    for name, v in (("gn_eps", GN_EPS), ("bn_eps", BN_EPS), ("root", -0.5), ("minus", -1.0)):
        put(name, np.full(P, v))
    return t


def kernel(x, L0_conv_w1, L0_conv_wg, L0_conv_w2, L1_conv_kernel, L2_conv_W_qk, L2_conv_b_qk, L2_conv_temperature,
           L3_conv_W1, L3_conv_b1, L3_conv_gamma, L3_conv_beta):
    import concourse.bacc as bacc
    from concourse.bass_utils import run_bass_kernel_spmd

    weights = [np.asarray(a) for a in (
        L0_conv_w1, L0_conv_wg, L0_conv_w2, L1_conv_kernel, L2_conv_W_qk, L2_conv_b_qk, L2_conv_temperature,
        L3_conv_W1, L3_conv_b1, L3_conv_gamma, L3_conv_beta)]
    choose = np.zeros((W // 4, G, W // 4, G, C), np.float32)
    for w in range(W // 4):
        for g in range(G):
            choose[w, g, w, g] = 1
    arrays = {"x": np.ascontiguousarray(x), "consts": constants(*weights), "choose": choose.reshape(P, W // 4, P)}
    nc = bacc.Bacc("TRN2", target_bir_lowering=False, num_devices=1)
    ins = [nc.dram_tensor(k, a.shape, mybir.dt.float32, kind="ExternalInput").ap() for k, a in arrays.items()]
    out = nc.dram_tensor("out", (B, H, W, C), mybir.dt.float32, kind="ExternalOutput").ap()
    build(nc, *ins, out)
    return run_bass_kernel_spmd(nc, [arrays], core_ids=[0]).results[0]["out"]
```

```python
import numpy as np
import concourse.bass as bass
from concourse import mybir
from contextlib import ExitStack

P = 128
B, H, W, C = 8, 128, 128, 32
G = P // C
NS = B // G
PIX = W * H
MULTI = 4
HEADS, WS = 4, 8
CK = C // HEADS
NWIN = W // WS
N = WS * WS
TAPS = 4
OW, OH = 5, 13
PW, PH = OW + TAPS - 1, OH + TAPS - 1
STRIPS = -(-W // OW)
PATCHES = -(-H // OH)
HPAD = OH * PATCHES + TAPS - 1
LAST_W = W - OW * (STRIPS - 1)
COLS = 96
K9 = 9
BANK = 512
RING = 2
DEEP = 4
ROWS = 8
GN_EPS, BN_EPS, LEAKY = 1e-5, 1e-3, 0.3

FIELDS = [
    ("ident", P), ("wg", MULTI * G * C), ("w2", C), ("fir", COLS), ("wk", P), ("temp", P), ("bk", P),
    ("keep", 2 * P), ("wq", HEADS * N), ("bq", (NWIN // 2) * P), ("w9", COLS), ("b9", G * K9),
    ("shift", 3 * P), ("mean8", P), ("w1", MULTI), ("gamma", 1), ("beta", 1), ("gn_eps", 1), ("bn_eps", 1),
    ("root", 1), ("minus", 1), 
]
AT, _n = {}, 0
for _name, _size in FIELDS:
    AT[_name] = (_n, _size)
    _n += _size
NCONST = _n


def build(nc, x, consts, choose, out):
    fp32 = mybir.dt.float32
    ALU = mybir.AluOpType
    ACT = mybir.ActivationFunctionType
    ds = bass.ds
    ctx = ExitStack()
    with ctx:
        def sb(name, cols):
            return ctx.enter_context(nc.sbuf_tensor(name, [P, cols], fp32))

        def sem(name):
            return ctx.enter_context(nc.semaphore(name))

        X = sb("X", NS * PIX)
        cst = sb("cst", NCONST)
        ST = sb("ST", NS * 4 * H)
        MW = NWIN * NWIN * (C + 1)
        work = sb("work", MW + 7168)
        stats = sb("stats", 64 * 6)
        mv = sb("mv", 2)
        co = sb("co", 16)
        l0s = sb("l0s", 2 * MULTI)
        vall = sb("vall", 4 * NS)
        bns = sb("bns", 16)
        ps = ctx.enter_context(nc.psum_tensor("ps", [P, 8, BANK], fp32))

        X3 = X[:, :].rearrange("p (w h) -> p w h", h=H)
        X5 = X[:, :].rearrange("p (b w h) -> p b w h", w=W // 4, h=H)
        X4 = X[:, :].rearrange("p (j w h) -> p j w h", w=NWIN, h=H)

        def c(name, rows=slice(0, P)):
            a, n = AT[name]
            return cst[rows, a:a + n]

        ident = c("ident")
        wg = c("wg").rearrange("p (j m o) -> p j m o", j=G, m=MULTI)
        wq = c("wq").rearrange("p (h n) -> p h n", h=HEADS)
        bq = c("bq").rearrange("p (q n) -> p q n", q=NWIN // 2)
        shift = c("shift").rearrange("p (k n) -> p k n", k=3)
        rstd, nmr, minus_mean = co[:, 0:1], co[:, 1:2], co[:, 2:3]
        ve = co[:, 3:4]

        def columns(s, w):
            return X5[:, ds(s * 4, 4), ds(w, 1), :].rearrange("p b o h -> p (b o) h")

        def rows4(v):
            return v.rearrange("p (b h) -> p b h", b=4)

        def part(at, shape):
            n = int(np.prod(shape))
            v = work[:, at:at + n]
            names = "abcdef"[:len(shape)]
            pat = "p (" + " ".join(names) + ") -> p " + " ".join(names)
            return v.rearrange(pat, **{k: s for k, s in zip(names[1:], shape[1:])}), at + n

        LOADS, LW = 4, 8
        stage, _e = part(0, [LOADS, G, LW * C])
        lined, _ = part(_e, [RING, LW, G, C])
        yb, _e = part(0, [RING, MULTI, 1024])
        zb, _ = part(_e, [RING, 2, BANK])
        strip, _e = part(0, [DEEP, HPAD, PW])
        patch, _ = part(_e, [RING, PATCHES, P])
        mall, _e0 = part(0, [NWIN, NWIN, C + 1])
        xn, _e = part(_e0, [RING, NWIN, WS, WS])
        xw, _e = part(_e, [RING, 4, P])
        kh, _e = part(_e, [RING, 4, G, P])
        mh, _e = part(_e0, [RING, NWIN, G, C])
        sums, _ = part(_e, [8, P])
        xs, _ = part(_e0, [NWIN, HEADS, NWIN])
        rs, _e = part(_e, [RING, 4, P])
        sT, _e = part(_e, [NWIN, P])
        T, _e = part(0, [W + 2, G * K9])
        xc, _e = part(_e, [DEEP, BANK])
        s_rows, _e = part(_e, [W * G])
        sel, _e = part(_e, [W // 4, P])
        vb, _ = part(_e, [DEEP, BANK])
        row, _o = part(0, [ROWS, BANK])
        assert _o <= (W + 2) * G * K9
        ob, _ = part(_e, [RING, G, 4, 4, C])

        ring_sems = {}

        def rsem(name, owner, ring=RING):
            s = sem(name)
            ring_sems.setdefault(owner, []).append((s, ring))
            return s

        def after(n, ring=RING):
            return n + 1 + ring

        def slot(n):
            return n + 1

        s_const = sem("consts_loaded")
        s_wk = sem("wk_scaled")
        s_stage = sem("stage_ended")
        s_passed = sem("wait_passed")
        s_load = [sem(f"chunk_loaded{u}") for u in range(LOADS)]
        s_lined = sem("chunk_lined_up")
        s_in = sem("bank_transposed")
        s_inst = sem("bank_measured")
        s_bank = sem("bank_copied")
        s_aggr = sem("moments_ready")
        s_pool = sem("pool_step")
        s_y = sem("y_ready")
        s_zp = sem("z_summed")
        s_zs = rsem("z_ready", "act")
        s_w2 = rsem("w2_summed", "pe")
        s_x1 = rsem("x1_written", "dve")
        s_strip = sem("strip_ready")
        s_zero = sem("buffers_zeroed")
        s_pt = sem("patches_transposed")
        s_pc = rsem("patches_copied", "act")
        s_cv = sem("half_filtered")
        s_x2 = rsem("x2_written", "dve")
        s_xn = sem("windows_normalised")
        s_wt = sem("windows_projected")
        s_xw = rsem("xw_ready", "act")
        s_kh = rsem("kh_ready", "dve")
        s_m = rsem("m_summed", "pe")
        s_mc = rsem("m_copied", "act")
        s_sp = sem("sums_projected")
        s_st = sem("sums_step")
        s_mh = sem("mh_ready")
        s_r = sem("r_summed")
        s_rc = rsem("r_copied", "act")
        s_xt = rsem("r_transposed", "pe")
        s_x3 = rsem("x3_written", "dve")
        s_xc = sem("x3n_ready")
        s_tp = rsem("t_projected", "pe", DEEP)
        s_td = rsem("t_stored", "dve", DEEP)
        s_sm = sem("s_summed")
        s_ss = sem("s_stored")
        s_sel = sem("sel_loaded")
        s_sc = sem("s_spread")
        s_v = rsem("v_ready", "dve", DEEP)
        s_g = sem("bn_step")
        s_fc = sem("out_s_spread")
        s_fv = rsem("out_v_ready", "dve", DEEP)
        s_fy = sem("out_y_ready")
        s_fl = sem("out_l_ready")
        s_fo = sem("out_sum_ready")
        s_ft = rsem("out_transposed", "pe", ROWS)
        s_fe = rsem("out_chunk_ready", "act", DEEP)
        s_out = [sem(f"chunk_stored{u}") for u in range(RING)]

        STAGES = 9
        ENG = 5

        def alone(eng):
            eng.sem_inc(s_passed, 1)

        def stage_end(eng, s, k):
            eng.drain().then_inc(s_stage, 1)
            eng.wait_ge(s_stage, s * (STAGES * ENG) + (k + 1) * ENG)
            alone(eng)

        def start_rings(eng, owner):
            for s, ring in ring_sems.get(owner, []):
                eng.sem_inc(s, ring)

        def spread_s(s, n, bank):
            return nc.tensor.matmul(ps[:, bank, :], sel[:, n, :], ST[:, ds(s * (4 * H), 4 * H)], start=True, stop=True)

        block = ctx.enter_context(nc.Block())

        @block.sync
        def _(sp):
            sp.dma_start(cst[:, :], consts[:, :]).then_inc(s_const, 16)
            with sp.Fori(0, NS) as s:
                def load(n, u):
                    sp.dma_start(stage[:, u, :, :],
                                 x[ds(s * G, G), :, ds(n * LW, LW), :].rearrange("g h w c -> h g (w c)")
                                 ).then_inc(s_load[u], 16)
                for u in range(LOADS):
                    load(u, u)
                with sp.Fori(1, W // LW // LOADS) as i:
                    for u in range(LOADS):
                        sp.wait_ge(s_lined, s * 16 + i * 4 + (u - 3))
                        alone(sp)
                        load(i * LOADS + u, u)
                for k in range(STAGES):
                    if k == 5:
                        sp.dma_start(sel[:, :, :], choose[:, :, :]).then_inc(s_sel, 16)
                    stage_end(sp, s, k)
            with sp.Fori(0, NS) as s:
                with sp.Fori(0, 4) as i:
                    for u in range(RING):
                        sp.wait_ge(s_fe, after(s * 32 + i * 8 + (4 * u + 3), DEEP))
                        for g in range(G):
                            o = out.rearrange("i h (b w) c -> h i b (w c)", b=4)
                            o = o[:, ds(s * G + g, 1), :, ds(i * (8 * C) + 4 * C * u, 4 * C)].rearrange("h a b w -> h (a b) w")
                            sp.dma_start(o, ob[:, u, g, :, :, :].rearrange("p b w c -> p b (w c)")).then_inc(s_out[u], 16)
            for u in range(RING):
                sp.wait_ge(s_out[u], NS * 4 * 64 + 64)

        @block.tensor
        def _(pe):
            start_rings(pe, "pe")
            pe.sem_inc(s_in, 2 * RING)
            pe.sem_inc(s_cv, 2 * RING)
            pe.sem_inc(s_r, 2 * RING)
            pe.wait_ge(s_const, 16)
            with pe.Fori(0, NS) as s:
                with pe.Fori(0, W // LW // LOADS) as i:
                    for u in range(LOADS):
                        pe.wait_ge(s_lined, s * 16 + i * 4 + (u + 1))
                        for b in range(2):
                            pe.wait_ge(s_bank, s * 32 + i * 8 + (2 * u + b + 1))
                            for w in range(4):
                                last = pe.transpose(ps[:, 2 * u + b, w * H:(w + 1) * H],
                                                    lined[:, u % 2, 4 * b + w, :, :].rearrange("p g c -> p (g c)"), ident)
                            last.then_inc(s_in, 1)
                stage_end(pe, s, 0)

                def wg_sum(i, q):
                    jp, hh, un = q % 2, (q // 2) % 2, q // 4
                    if q % 4 == 0:
                        pe.wait_ge(s_y, s * 16 + i * 2 + (un + 1))
                    pe.wait_ge(s_zs, slot(s * 64 + i * 8 + q))
                    for jj in range(2):
                        for m in range(MULTI):
                            last = pe.matmul(ps[C * m:C * m + C, 2 * (q % 2) + jj, :], wg[:, 2 * jp + jj, m, :],
                                             yb[:, un, m, BANK * hh:BANK * hh + BANK], start=True, stop=True)
                    last.then_inc(s_zp, 1)

                def w2_sum(i, q):
                    jp, hh = q % 2, (q // 2) % 2
                    pe.wait_ge(s_zs, after(s * 64 + i * 8 + q))
                    if jp == 0:
                        pe.wait_ge(s_x1, slot(s * 32 + i * 4 + q // 2))
                    for jj in range(2):
                        j = 2 * jp + jj
                        last = pe.matmul(ps[C * j:C * j + C, 4 + hh, :], c("w2"), zb[:, q % 2, jj, :],
                                         start=True, stop=True)
                    last.then_inc(s_w2, 1)

                for q in range(8):
                    wg_sum(0, q)
                    if q:
                        w2_sum(0, q - 1)
                with pe.Fori(1, 8) as i:
                    for q in range(8):
                        wg_sum(i, q)
                        w2_sum(i, q - 1)
                w2_sum(7, 7)
                stage_end(pe, s, 1)

                def to_patches(t, u):
                    pe.wait_ge(s_strip, s * STRIPS + t + 1)
                    pe.wait_ge(s_pc, slot(s * STRIPS + t))
                    for k in range(PATCHES):
                        at = 3 * BANK * (u % 2) + k * P
                        last = pe.transpose(ps[:, at // BANK, at % BANK:at % BANK + P],
                                            strip[:, u, OH * k:OH * k + PH, :].rearrange("p h w -> p (h w)"), ident)
                    last.then_inc(s_pt, 1)

                def filtered(t, u):
                    pe.wait_ge(s_pc, after(s * STRIPS + t))
                    for hf in range(2):
                        pe.wait_ge(s_x2, slot(s * (2 * STRIPS) + t * 2 + hf))
                        for k in range(PATCHES // 2):
                            last = pe.matmul(ps[:, 6 + hf, COLS * k:COLS * k + COLS],
                                             patch[:, u % 2, hf * (PATCHES // 2) + k, :], c("fir"), start=True, stop=True)
                        last.then_inc(s_cv, 1)

                to_patches(0, 0)
                with pe.Fori(0, STRIPS // DEEP) as i:
                    for u in range(DEEP):
                        to_patches(i * DEEP + (u + 1), (u + 1) % DEEP)
                        filtered(i * DEEP + u, u)
                for t in range(STRIPS // DEEP * DEEP, STRIPS):
                    if t + 1 < STRIPS:
                        to_patches(t + 1, (t + 1) % DEEP)
                    filtered(t, t % DEEP)
                stage_end(pe, s, 2)

                def project(w1, n, xu, hf):
                    nn = s * 32 + n
                    if hf == 0:
                        pe.wait_ge(s_xn, s * 16 + w1 + 1)
                    pe.wait_ge(s_xw, slot(nn))
                    pe.wait_ge(s_kh, slot(nn))
                    for what, bank in ((ident, 0), (c("wk"), 2)):
                        for pp in range(4):
                            h1 = 2 * (4 * hf + pp)
                            px = xn[:, xu, h1:h1 + 2, :, :].rearrange("p h j i -> p (h j i)")
                            o = ps[:, bank + hf, pp * P:pp * P + P]
                            if bank == 0:
                                pe.transpose(o, px, what)
                            else:
                                last = pe.matmul(o, px, what, start=True, stop=True)
                    last.then_inc(s_wt, 1)

                def m_sum(n, u):
                    nn = s * 32 + n
                    pe.wait_ge(s_xw, after(nn))
                    pe.wait_ge(s_kh, after(nn))
                    pe.wait_ge(s_mc, slot(nn))
                    for pp in range(4):
                        for g in range(G):
                            last = pe.matmul(ps[C * g:C * g + C, 4 + u, pp * P:pp * P + P],
                                             xw[:, u, pp, C * g:C * g + C], kh[:, u, pp, g, :],
                                             start=True, stop=True)
                    last.then_inc(s_m, 1)

                project(0, 0, 0, 0)
                project(0, 1, 0, 1)
                m_sum(0, 0)
                with pe.Fori(0, 7) as i:
                    for u in range(2):
                        w1 = i * 2 + (u + 1)
                        project(w1, w1 * 2, 1 - u, 0)
                        m_sum(w1 * 2 - 1, 1)
                        project(w1, w1 * 2 + 1, 1 - u, 1)
                        m_sum(w1 * 2, 0)
                project(15, 30, 1, 0)
                m_sum(29, 1)
                project(15, 31, 1, 1)
                m_sum(30, 0)
                m_sum(31, 1)
                pe.wait_ge(s_st, s * 2 + 1)
                for pr in range(NWIN // 2):
                    v = xs[:, 2 * pr:2 * pr + 2, :, :].rearrange("p a b c -> p (a b c)")
                    last = pe.matmul(ps[:, 6 + pr // 4, (pr % 4) * P:(pr % 4) * P + P], v, c("wk"), start=True, stop=True)
                last.then_inc(s_sp, 1)
                stage_end(pe, s, 3)

                def r_sum(w1, n, mu, hf):
                    nn = s * 32 + n
                    if hf == 0:
                        pe.wait_ge(s_mh, s * 16 + w1 + 1)
                    pe.wait_ge(s_rc, slot(nn))
                    for q in range(4):
                        pe.matmul(ps[:, hf, q * P:q * P + P], bq[:, 4 * hf + q, :],
                                  sT[:, ds(w1, 1), :].rearrange("p a b -> p (a b)"), start=(q == 0), stop=False)
                    for hp in range(2):
                        for hd in range(HEADS):
                            mvg = mh[:, mu, 8 * hf + hp:8 * hf + hp + 7:2, :, hd * CK:hd * CK + CK]
                            o = ps[N * hp:N * hp + N, hf, :].rearrange("p (q g d) -> p q g d", q=4, g=G)
                            last = pe.matmul(o[:, :, :, hd * CK:hd * CK + CK], wq[:, hd, :], mvg,
                                             start=False, stop=(hd == HEADS - 1))
                    last.then_inc(s_r, 1)

                def r_back(n, u):
                    nn = s * 32 + n
                    pe.wait_ge(s_rc, after(nn))
                    pe.wait_ge(s_x3, slot(nn))
                    for q in range(4):
                        last = pe.transpose(ps[:, 2 + u, q * P:q * P + P], rs[:, u, q, :], ident)
                    last.then_inc(s_xt, 1)

                r_sum(0, 0, 0, 0)
                r_sum(0, 1, 0, 1)
                r_back(0, 0)
                with pe.Fori(0, 7) as i:
                    for u in range(2):
                        w1 = i * 2 + (u + 1)
                        r_sum(w1, w1 * 2, 1 - u, 0)
                        r_back(w1 * 2 - 1, 1)
                        r_sum(w1, w1 * 2 + 1, 1 - u, 1)
                        r_back(w1 * 2, 0)
                r_sum(15, 30, 1, 0)
                r_back(29, 1)
                r_sum(15, 31, 1, 1)
                r_back(30, 0)
                r_back(31, 1)
                stage_end(pe, s, 4)

                with pe.Fori(0, 8) as i:
                    for u in range(DEEP):
                        nn = s * 32 + i * DEEP + u
                        pe.wait_ge(s_xc, nn + 1)
                        pe.wait_ge(s_td, slot(nn))
                        for w in range(4):
                            last = pe.matmul(ps[:, u, w * COLS:w * COLS + COLS], xc[:, u, w * H:w * H + H], c("w9"),
                                             start=True, stop=True)
                        last.then_inc(s_tp, 1)
                stage_end(pe, s, 5)
                for k in range(K9):
                    ki, kj = divmod(k, 3)
                    mvg = T[:, 2 - kj:2 - kj + W, :].rearrange("p w (g k) -> p w g k", k=K9)[:, :, :, k]
                    last = pe.matmul(ps[:, 7, :], shift[:, ki, :], mvg, start=(k == 0), stop=(k == K9 - 1))
                last.then_inc(s_sm, 1)
                pe.wait_ge(s_ss, s + 1)
                for b in range(4):
                    last = pe.transpose(ps[:, 6, b * H:b * H + H], s_rows[:, b * P:b * P + P], ident)
                last.then_inc(s_sm, 1)
                stage_end(pe, s, 6)
                pe.wait_ge(s_sel, s * 16 + 16)
                for n in range(32):
                    pe.wait_ge(s_v, slot(s * 32 + n))
                    spread_s(s, n, n % DEEP).then_inc(s_sc, 1)
                stage_end(pe, s, 7)
                stage_end(pe, s, 8)
            pe.wait_ge(s_g, 2)
            pe.matmul(ps[:, DEEP, 0:NS], c("mean8"), bns[:, 0:2], start=True, stop=True).then_inc(s_g, 1)
            pe.wait_ge(s_g, 7)
            pe.matmul(ps[:, DEEP + 1, 0:NS], c("mean8"), bns[:, 4:6], start=True, stop=True).then_inc(s_g, 1)
            with pe.Fori(0, NS) as s:
                def out_s(n):
                    pe.wait_ge(s_fv, slot(s * 32 + n))
                    spread_s(s, n, n % DEEP).then_inc(s_fc, 1)

                def out_t(n):
                    nn = s * 32 + n
                    pe.wait_ge(s_fo, nn + 1)
                    pe.wait_ge(s_fe, slot(nn))
                    for w in range(4):
                        last = pe.transpose(ps[:, DEEP + n % DEEP, w * P:w * P + P], row[:, n % ROWS, w * H:w * H + H],
                                            ident)
                    last.then_inc(s_ft, 1)

                for n in range(DEEP + 1):
                    out_s(n)
                for n in range(32):
                    if n + DEEP + 1 < 32:
                        out_s(n + DEEP + 1)
                    out_t(n)

        @block.scalar
        def _(act):
            start_rings(act, "act")
            act.sem_inc(s_bank, 8)
            act.sem_inc(s_out[0], 64)
            act.sem_inc(s_out[1], 64)
            with act.Fori(0, NS) as s:
                with act.Fori(0, 4) as i:
                    for b in range(8):
                        act.wait_ge(s_inst, s * 32 + i * 8 + b + 1)
                        act.activation(X[:, ds(s * PIX + i * 8 * BANK + b * BANK, BANK)], ps[:, b, :], ACT.Copy
                                       ).then_inc(s_bank, 1)
                stage_end(act, s, 0)

                def gelu_y(n, u, m):
                    o = act.activation(yb[:, u, m, :], X[:, ds(s * PIX + n * 1024, 1024)], ACT.Gelu,
                                       scale=l0s[:, m:m + 1], bias=l0s[:, MULTI + m:MULTI + m + 1])
                    if m == MULTI - 1:
                        o.then_inc(s_y, 1)

                def gelu_z(i, q):
                    nn = s * 64 + i * 8 + q
                    act.wait_ge(s_zp, nn + 1)
                    act.wait_ge(s_w2, slot(nn))
                    act.activation(zb[:, q % 2, :, :].rearrange("p a b -> p (a b)"),
                                   ps[:, 2 * (q % 2):2 * (q % 2) + 2, :].rearrange("p a b -> p (a b)"),
                                   ACT.Gelu).then_inc(s_zs, 1)

                def gates(i, last=False):
                    for un in range(2):
                        nxt = not (last and un == 1)
                        for pc in range(4):
                            gelu_z(i, 4 * un + pc)
                            if nxt:
                                for m in ((0, 1), (2,), (3,), ())[pc]:
                                    gelu_y(i * 2 + (un + 1), 1 - un, m)

                for m in range(MULTI):
                    gelu_y(0, 0, m)
                with act.Fori(0, 7) as i:
                    gates(i)
                gates(7, last=True)
                stage_end(act, s, 1)

                with act.Fori(0, STRIPS // 2) as i:
                    for u in range(2):
                        nn = s * STRIPS + i * 2 + u
                        act.wait_ge(s_pt, nn + 1)
                        act.wait_ge(s_cv, nn * 2 + 2)
                        act.activation(patch[:, u, :, :].rearrange("p a b -> p (a b)"),
                                       ps[:, 3 * u:3 * u + 3, :].rearrange("p a b -> p (a b)")[:, 0:PATCHES * P],
                                       ACT.Copy).then_inc(s_pc, 1)
                stage_end(act, s, 2)

                def copy_xw(n, u):
                    nn = s * 32 + n
                    act.wait_ge(s_wt, nn + 1)
                    act.wait_ge(s_m, slot(nn))
                    act.activation(xw[:, u, :, :].rearrange("p a b -> p (a b)"), ps[:, u, :], ACT.Copy
                                   ).then_inc(s_xw, 1)

                def copy_m(n, u):
                    nn = s * 32 + n
                    act.wait_ge(s_m, after(nn))
                    src = ps[:, 4 + u, :].rearrange("p (a b) -> p a b", b=N)[:, :, 0:C + 1]
                    dst = work[:, ds(n * (8 * (C + 1)), 8 * (C + 1))].rearrange("p (a b) -> p a b", b=C + 1)
                    act.activation(dst, src, ACT.Copy).then_inc(s_mc, 1)

                copy_xw(0, 0)
                with act.Fori(0, 15) as i:
                    for u in range(2):
                        copy_xw(i * 2 + (u + 1), 1 - u)
                        copy_m(i * 2 + u, u)
                copy_xw(31, 1)
                copy_m(30, 0)
                copy_m(31, 1)
                stage_end(act, s, 3)

                def spread_m(w1, u):
                    act.wait_ge(s_r, s * 32 + w1 * 2 + 2)
                    for g in range(G):
                        src = work[C * g:C * g + C, ds(w1 * (NWIN * (C + 1)), NWIN * (C + 1))
                                   ].rearrange("p (a b) -> p a b", b=C + 1)[:, :, 0:C]
                        last = act.activation(mh[C * g:C * g + C, u, :, g, :], src, ACT.Copy)
                    last.then_inc(s_mh, 1)

                def copy_r(n, u):
                    nn = s * 32 + n
                    act.wait_ge(s_r, after(nn) + RING)
                    act.wait_ge(s_xt, slot(nn))
                    act.activation(rs[:, u, :, :].rearrange("p a b -> p (a b)"), ps[:, u, :], ACT.Copy
                                   ).then_inc(s_rc, 1)

                act.wait_ge(s_zero, s * 3 + 3)
                spread_m(0, 0)
                with act.Fori(0, 7) as i:
                    for u in range(2):
                        w1 = i * 2 + u
                        spread_m(w1 + 1, 1 - u)
                        copy_r(w1 * 2, 0)
                        copy_r(w1 * 2 + 1, 1)
                spread_m(15, 1)
                for n in range(28, 32):
                    copy_r(n, n % 2)
                stage_end(act, s, 4)

                with act.Fori(0, 8) as i:
                    for u in range(DEEP):
                        nn = s * 32 + i * DEEP + u
                        act.wait_ge(s_tp, slot(nn))
                        act.activation(xc[:, u, :], X[:, ds(s * PIX + i * (DEEP * BANK) + u * BANK, BANK)], ACT.Identity,
                                       scale=rstd, bias=nmr).then_inc(s_xc, 1)
                for k in range(5, STAGES):
                    stage_end(act, s, k)
            for s in range(NS):
                def norm(n, u):
                    act.wait_ge(s_fv, after(s * 32 + n, DEEP))
                    act.activation(row[:, u, :], row[:, u, :], ACT.Identity, scale=bns[:, 12 + s:13 + s],
                                   bias=bns[:, 15:16]).then_inc(s_fy, 1)

                def lay(n, j, k, i):
                    act.wait_ge(s_ft, after(s * 32 + n, ROWS))
                    if j == 0:
                        act.wait_ge(s_out[k], s * 256 + i * 64 + 64)
                    o = ob[:, k, :, :, j, :].rearrange("p g b c -> p b g c")
                    act.activation(o, ps[:, DEEP + j, :].rearrange("p (b g c) -> p b g c", b=4, g=G), ACT.Copy
                                   ).then_inc(s_fe, 1)

                LEAD = 4
                for n in range(LEAD):
                    norm(n, n)
                with act.Fori(0, 3) as i:
                    for j in range(8):
                        norm(i * 8 + (j + LEAD), (j + LEAD) % ROWS)
                        lay(i * 8 + j, j % 4, j // 4, i)
                for j in range(8):
                    if j + LEAD < 8:
                        norm(24 + j + LEAD, j + LEAD)
                    lay(24 + j, j % 4, j // 4, 3)

        @block.vector
        def _(dve):
            start_rings(dve, "dve")
            dve.wait_ge(s_const, 16)
            dve.tensor_tensor(c("wk"), c("wk"), c("temp"), ALU.mult)
            dve.tensor_tensor(c("bk"), c("bk"), c("temp"), ALU.mult).then_inc(s_wk, 1)
            dve.wait_ge(s_wk, 1)
            with dve.Fori(0, NS) as s:
                def measure(i, u):
                    for b in range(2 * u, 2 * u + 2):
                        dve.wait_ge(s_in, after(s * 32 + i * 8 + b) + RING)
                        dve.bn_stats(stats[:, ds(i * 48 + 6 * b, 6)], ps[:, b, :]).then_inc(s_inst, 1)

                def moments(n):
                    dve.drain()
                    dve.bn_aggr(mv[:, :], stats[:, 0:6 * n]).then_inc(s_aggr, 1)

                with dve.Fori(0, 4) as i:
                    for u in range(LOADS):
                        dve.wait_ge(s_load[u], s * 64 + i * 16 + 16)
                        dve.wait_ge(s_in, s * 32 + i * 8 + (2 * u + 2))
                        dve.tensor_copy(lined[:, u % 2, :, :, :],
                                        stage[:, u, :, :].rearrange("p g (w c) -> p w g c", c=C)).then_inc(s_lined, 1)
                        if u:
                            measure(i, u - 1)
                    measure(i, LOADS - 1)
                moments(32)
                stage_end(dve, s, 0)

                with dve.Fori(0, 8) as i:
                    def bank(u):
                        return X[:, ds(s * PIX + i * (4 * BANK) + u * BANK, BANK)]

                    def measure_x1(u):
                        dve.wait_ge(s_x1, after(s * 32 + i * 4 + u))
                        alone(dve)
                        dve.bn_stats(stats[:, ds(i * 24 + 6 * u, 6)], bank(u))

                    for u in range(4):
                        dve.wait_ge(s_w2, after((s * 32 + i * 4 + u) * 2 + 1))
                        dve.tensor_tensor(bank(u), bank(u), ps[:, 4 + u % 2, :], ALU.add).then_inc(s_x1, 1)
                        if u:
                            measure_x1(u - 1)
                    measure_x1(3)
                moments(32)
                stage_end(dve, s, 1)

                def norm_strip(t, u, lo, hi):
                    o = strip[:, u, 1:1 + H, lo:hi].rearrange("p h w -> p w h")
                    dve.tensor_scalar(o, X3[:, ds(s * W + t * OW + (lo - 1), hi - lo), :], rstd, nmr,
                                      ALU.mult, ALU.add).then_inc(s_strip, 1)

                half = OH * PATCHES // 2

                def add_filtered(t, u, ow):
                    nn = s * (2 * STRIPS) + t * 2
                    w0 = s * W + t * OW
                    for hf in range(2):
                        dve.wait_ge(s_cv, after(nn + hf) + RING)
                        rows = ((0, 5),) if hf == 0 else ((0, 4), (4, 5))
                        for k0, k1 in rows:
                            h0 = hf * half + k0 * OH
                            nk, nh = k1 - k0, min(OH, H - h0)
                            src = ps[:, 6 + hf, 0:5 * COLS].rearrange("p (k n) -> p k n", n=COLS)[:, k0:k1, 0:ow * OH]
                            src = src.rearrange("p k (w h) -> p w k h", h=OH)[:, :, :, 0:nh]
                            v = X3[:, ds(w0, ow), h0:h0 + nk * nh].rearrange("p w (k h) -> p w k h", h=nh)
                            last = dve.tensor_tensor(v, v, src, ALU.add)
                        last.then_inc(s_x2, 1)

                def measure_x2(t, ow):
                    w0 = s * W + t * OW
                    dve.wait_ge(s_x2, after((s * STRIPS + t) * 2 + 1))
                    alone(dve)
                    for hf, (a, b) in enumerate(((0, half), (half, H))):
                        dve.bn_stats(stats[:, ds(t * 12 + 6 * hf, 6)], X3[:, ds(w0, ow), a:b])

                dve.wait_ge(s_zero, s * 3 + 1)
                norm_strip(0, 0, 1, PW)
                for t in range(1, DEEP - 1):
                    norm_strip(t, t, 0, PW)
                peeled = (STRIPS - DEEP) // DEEP * DEEP
                with dve.Fori(0, peeled // DEEP) as i:
                    for u in range(DEEP):
                        add_filtered(i * DEEP + u, u, OW)
                        norm_strip(i * DEEP + (u + DEEP - 1), (u + DEEP - 1) % DEEP, 0, PW)
                        measure_x2(i * DEEP + u, OW)
                for t in range(peeled, STRIPS):
                    ow = OW if t < STRIPS - 1 else LAST_W
                    add_filtered(t, t % DEEP, ow)
                    nxt = t + DEEP - 1
                    if nxt < STRIPS - 1:
                        norm_strip(nxt, nxt % DEEP, 0, PW)
                    if nxt == STRIPS - 1:
                        dve.memset(strip[:, nxt % DEEP, 1:1 + H, LAST_W + 1:PW], 0.0)
                        norm_strip(nxt, nxt % DEEP, 0, LAST_W + 1)
                    measure_x2(t, ow)
                moments(2 * STRIPS)
                stage_end(dve, s, 2)

                def norm_windows(w1, u):
                    dve.tensor_scalar(xn[:, u, :, :, :].rearrange("p h j i -> p j i h"),
                                      X4[:, ds(s * 8, 8), ds(w1, 1), :].rearrange("p j a (i h) -> p (j a) i h", i=WS),
                                      rstd, nmr, ALU.mult, ALU.add).then_inc(s_xn, 1)

                def keys(n, u):
                    nn = s * 32 + n
                    dve.wait_ge(s_wt, nn + 1)
                    dve.wait_ge(s_m, slot(nn))
                    for hp in range(2):
                        rows = slice(N * hp, N * hp + N)
                        k_in = ps[rows, 2 + u, :].rearrange("p (a g d) -> p a g d", a=4, g=G)
                        bias = c("bk", rows).rearrange("p (o g d) -> p o g d", o=1, g=G).broadcast_to([N, 4, G, C])
                        o = kh[rows, u, :, :, N * hp:N * hp + C]
                        last = dve.tensor_tensor(o, k_in, bias, ALU.add)
                    last.then_inc(s_kh, 1)

                dve.wait_ge(s_zero, s * 3 + 2)
                norm_windows(0, 0)
                norm_windows(1, 1)
                with dve.Fori(0, 7) as i:
                    for u in range(2):
                        w1 = i * 2 + u
                        keys(w1 * 2, 0)
                        keys(w1 * 2 + 1, 1)
                        norm_windows(w1 + 2, u)
                for n in range(28, 32):
                    keys(n, n % 2)
                dve.wait_ge(s_mc, after(s * 32 + 31))
                dve.tensor_copy(xs[:, :, :, :], mall[:, :, :, C:C + 1].rearrange("p a b o -> p a o b"
                                                                                ).broadcast_to([P, NWIN, HEADS, NWIN])
                                ).then_inc(s_st, 1)
                dve.wait_ge(s_sp, s + 1)
                dve.scalar_tensor_tensor(
                    sums, c("bk").rearrange("p (o n) -> p o n", o=1).broadcast_to([P, 8, P]), float(N),
                    ps[:, 6:8, :].rearrange("p a (b n) -> p (a b) n", n=P), ALU.mult, ALU.add).then_inc(s_st, 1)
                dve.wait_ge(s_st, s * 2 + 2)
                for par in range(2):
                    keep = c("keep")[:, par * P:par * P + P].rearrange("p (o n) -> p o n", o=1).broadcast_to([P, 8, P])
                    dve.tensor_tensor(sT[:, par:NWIN:2, :], sums, keep, ALU.mult)
                stage_end(dve, s, 3)

                with dve.Fori(0, 16) as i:
                    def half_windows(hf):
                        return X3[:, ds(s * W + i * WS, WS), 64 * hf:64 * hf + 64]

                    def measure_x3(hf):
                        dve.wait_ge(s_x3, after(s * 32 + i * 2 + hf))
                        alone(dve)
                        dve.bn_stats(stats[:, ds(i * 12 + 6 * hf, 6)], half_windows(hf))

                    for hf in range(2):
                        nn = s * 32 + i * 2 + hf
                        dve.wait_ge(s_xt, after(nn))
                        v = half_windows(hf)
                        src = ps[:, 2 + hf, :].rearrange("p (q j i) -> p j q i", j=WS, i=WS)
                        v4 = v.rearrange("p j (q i) -> p j q i", i=WS)
                        dve.tensor_tensor(v4, v4, src, ALU.add).then_inc(s_x3, 1)
                        if hf:
                            measure_x3(0)
                    measure_x3(1)
                moments(32)
                stage_end(dve, s, 4)

                with dve.Fori(0, 8) as i:
                    for u in range(DEEP):
                        nn = s * 32 + i * DEEP + u
                        dve.wait_ge(s_tp, after(nn, DEEP))
                        o = T[:, ds(i * (4 * DEEP) + 4 * u + 1, 4), :]
                        bias = c("b9").rearrange("p (o n) -> p o n", o=1).broadcast_to([P, 4, G * K9])
                        src = ps[:, u, 0:4 * COLS].rearrange("p (w n) -> p w n", n=COLS)[:, :, 0:G * K9]
                        dve.tensor_tensor(o, src, bias, ALU.add).then_inc(s_td, 1)
                dve.drain()
                dve.memset(T[:, 0:2, :], 0.0)
                dve.memset(T[:, W:W + 2, :], 0.0)
                stage_end(dve, s, 5)
                dve.wait_ge(s_sm, s * 2 + 1)
                dve.tensor_copy(s_rows[:, :], ps[:, 7, :]).then_inc(s_ss, 1)
                dve.wait_ge(s_sm, s * 2 + 2)
                dve.tensor_copy(ST[:, ds(s * (4 * H), 4 * H)], ps[:, 6, :])
                stage_end(dve, s, 6)
                with dve.Fori(0, 8) as i:
                    def measure_v(u):
                        dve.wait_ge(s_v, after(s * 32 + i * DEEP + u, DEEP))
                        alone(dve)
                        dve.bn_stats(stats[:, ds(i * (6 * DEEP) + 6 * u, 6)], vb[:, u, :])

                    for u in range(DEEP):
                        dve.wait_ge(s_sc, s * 32 + i * DEEP + (u + 1))
                        dve.scalar_tensor_tensor(rows4(vb[:, u, :]), columns(s, i * DEEP + u), minus_mean,
                                                 rows4(ps[:, u, :]), ALU.add, ALU.mult).then_inc(s_v, 1)
                        if u:
                            measure_v(u - 1)
                    measure_v(DEEP - 1)
                moments(32)
                stage_end(dve, s, 7)
                dve.tensor_copy(vall[:, ds(s * 4, 2)], mv[:, :])
                dve.tensor_copy(vall[:, ds(s * 4 + 2, 1)], rstd)
                dve.tensor_copy(vall[:, ds(s * 4 + 3, 1)], minus_mean)
                stage_end(dve, s, 8)
            dve.wait_ge(s_g, 3)
            va = vall[:, :].rearrange("p (s k) -> p k s", k=4)
            steps = [3]

            def step(ins):
                ins.then_inc(s_g, 1)
                steps[0] += 1
                dve.wait_ge(s_g, steps[0])

            step(dve.tensor_reduce(bns[:, 8:9], ps[:, DEEP, 0:NS], mybir.AxisListType.X, ALU.add))
            step(dve.tensor_scalar(bns[:, 4:6], bns[:, 0:2], bns[:, 8:9], None, ALU.subtract))
            step(dve.tensor_tensor(bns[:, 4:6], bns[:, 4:6], bns[:, 4:6], ALU.mult))
            dve.tensor_tensor(bns[:, 4:6], bns[:, 4:6], bns[:, 2:4], ALU.add).then_inc(s_g, 1)
            dve.wait_ge(s_g, 8)
            steps[0] = 8
            step(dve.tensor_reduce(bns[:, 9:10], ps[:, DEEP + 1, 0:NS], mybir.AxisListType.X, ALU.add))
            dve.wait_ge(s_g, 11)
            steps[0] = 11
            step(dve.tensor_tensor(bns[:, 11:12], bns[:, 10:11], c("gamma"), ALU.mult))
            step(dve.tensor_tensor(bns[:, 12:14], va[:, 2, :], bns[:, 11:12].broadcast_to([P, 2]), ALU.mult))
            step(dve.tensor_tensor(bns[:, 14:15], bns[:, 8:9], bns[:, 11:12], ALU.mult))
            step(dve.tensor_tensor(bns[:, 15:16], c("beta"), bns[:, 14:15], ALU.subtract))
            for s in range(NS):
                def scaled(n, u):
                    dve.wait_ge(s_fc, n + (s * 32 + 1))
                    dve.wait_ge(s_ft, slot(n + s * 32))
                    dve.scalar_tensor_tensor(rows4(row[:, u, :]), columns(s, n), vall[:, 4 * s + 3:4 * s + 4],
                                             rows4(ps[:, u % DEEP, :]), ALU.add, ALU.mult).then_inc(s_fv, 1)

                def leaky(n, u):
                    dve.wait_ge(s_fy, n + (s * 32 + 1))
                    dve.scalar_tensor_tensor(row[:, u, :], row[:, u, :], LEAKY, row[:, u, :], ALU.mult, ALU.max
                                             ).then_inc(s_fl, 1)

                scaled(0, 0)
                scaled(1, 1)
                with dve.Fori(0, 32 // ROWS - 1) as i:
                    for u in range(ROWS):
                        scaled(i * ROWS + (u + 2), (u + 2) % ROWS)
                        leaky(i * ROWS + u, u)
                for n in range(32 - ROWS, 32):
                    if n + 2 < 32:
                        scaled(n + 2, (n + 2) % ROWS)
                    leaky(n, n % ROWS)

        @block.gpsimd
        def _(pool):
            start_rings(pool, "pool")
            pool.wait_ge(s_const, 16)
            PS = 18

            with pool.Fori(0, NS) as s:
                cnt = [0]

                def step(ins):
                    cnt[0] += 1
                    ins.then_inc(s_pool, 1)
                    pool.wait_ge(s_pool, s * PS + cnt[0])
                    alone(pool)

                def coefficients(k):
                    pool.wait_ge(s_aggr, s * 5 + k + 1)
                    step(pool.tensor_tensor(ve, mv[:, 1:2], c("gn_eps"), ALU.add))
                    step(pool.tensor_tensor(rstd, ve, c("root"), ALU.pow))
                    step(pool.tensor_tensor(minus_mean, mv[:, 0:1], c("minus"), ALU.mult))
                    step(pool.tensor_tensor(nmr, minus_mean, rstd, ALU.mult))

                coefficients(0)
                step(pool.tensor_tensor(l0s[:, 0:MULTI], c("w1"), rstd.broadcast_to([P, MULTI]), ALU.mult))
                step(pool.tensor_tensor(l0s[:, MULTI:2 * MULTI], c("w1"), nmr.broadcast_to([P, MULTI]), ALU.mult))
                stage_end(pool, s, 0)
                coefficients(1)
                stage_end(pool, s, 1)
                pool.memset(strip[:, :, :, :], 0.0).then_inc(s_zero, 1)
                coefficients(2)
                stage_end(pool, s, 2)
                pool.memset(kh[:, :, :, :, :], 0.0)
                pool.drain()
                for hp in range(2):
                    last = pool.memset(kh[N * hp:N * hp + N, :, :, :, N * hp + C:N * hp + C + 1], 1.0)
                last.then_inc(s_zero, 1)
                stage_end(pool, s, 3)
                pool.memset(mh[:, :, :, :, :], 0.0).then_inc(s_zero, 1)
                coefficients(3)
                assert cnt[0] == PS
                stage_end(pool, s, 4)
                stage_end(pool, s, 5)
                stage_end(pool, s, 6)
                stage_end(pool, s, 7)
                stage_end(pool, s, 8)
            va = vall[:, :].rearrange("p (s k) -> p k s", k=4)
            pool.tensor_tensor(bns[:, 0:2], va[:, 0, :], va[:, 2, :], ALU.mult).then_inc(s_g, 1)
            pool.tensor_tensor(bns[:, 2:4], va[:, 1, :], va[:, 2, :], ALU.mult)
            pool.drain()
            pool.tensor_tensor(bns[:, 2:4], bns[:, 2:4], va[:, 2, :], ALU.mult).then_inc(s_g, 1)
            pool.wait_ge(s_g, 9)
            pool.tensor_tensor(bns[:, 10:11], bns[:, 9:10], c("bn_eps"), ALU.add).then_inc(s_g, 1)
            pool.wait_ge(s_g, 10)
            pool.tensor_tensor(bns[:, 10:11], bns[:, 10:11], c("root"), ALU.pow).then_inc(s_g, 1)
            with pool.Fori(0, NS) as s:
                with pool.Fori(0, 32 // ROWS) as i:
                    for u in range(ROWS):
                        n = i * ROWS + u
                        pool.wait_ge(s_fl, s * 32 + i * ROWS + (u + 1))
                        pool.tensor_tensor(rows4(row[:, u, :]), columns(s, n), rows4(row[:, u, :]), ALU.add
                                           ).then_inc(s_fo, 1)


def constants(w1, wg, w2, fir, W_qk, b_qk, temperature, W9, b9, gamma, beta):
    t = np.zeros((P, NCONST), np.float32)

    def put(name, a):
        at, n = AT[name]
        t[:, at:at + n] = np.asarray(a, np.float32).reshape(P, n)

    put("ident", np.eye(P))
    a = np.zeros((G, C, G, MULTI, C), np.float32)
    for j in range(G):
        a[j, :, j] = wg.transpose(2, 0, 1)
    put("wg", a)
    a = np.zeros((MULTI, C, C), np.float32)
    for m in range(MULTI):
        a[m, range(C), range(C)] = w2[:, m]
    put("w2", a)
    a = np.zeros((PH, PW, COLS), np.float32)
    for w in range(OW):
        for h in range(OH):
            a[h:h + TAPS, w:w + TAPS, w * OH + h] = fir
    put("fir", a)
    a = np.zeros((G, C, G, C), np.float32)
    for g in range(G):
        a[g, :, g] = W_qk[N * HEADS:].T
    put("wk", a)
    heads = np.repeat(temperature, CK)
    put("temp", np.broadcast_to(np.tile(heads, G), (P, P)))
    put("bk", np.broadcast_to(np.tile(b_qk[N * HEADS:], G), (P, P)))
    a = np.zeros((2, HEADS, NWIN, 2, G, HEADS, CK), np.float32)
    for par in range(2):
        for hd in range(HEADS):
            a[par, hd, :, par, :, hd] = 1
    put("keep", a)
    q = W_qk[:N * HEADS].reshape(HEADS, WS, WS, C).transpose(3, 0, 2, 1)
    put("wq", np.broadcast_to(q[None], (G, C, HEADS, WS, WS)))
    bq = b_qk[:N * HEADS].reshape(HEADS, WS, WS).transpose(0, 2, 1).reshape(HEADS, N)
    a = np.zeros((2, HEADS, NWIN, NWIN // 2, 2, N), np.float32)
    for h1 in range(NWIN):
        a[:, :, h1, h1 // 2, h1 % 2] = bq
    put("bq", a)
    a = np.zeros((G, C, COLS), np.float32)
    for g in range(G):
        a[g, :, g * K9:(g + 1) * K9] = W9
    put("w9", a)
    put("b9", np.broadcast_to(np.tile(b9, G), (P, G * K9)))
    a = np.zeros((P, 3, P), np.float32)
    for k in range(3):
        for h in range(1, H - 1):
            a[h, k, h + k - 1] = 1
    put("shift", a)
    put("mean8", np.tile(np.eye(C), (G, G)) / B)
    put("w1", np.tile(w1, (G, 1)))
    put("gamma", np.tile(gamma, G))
    put("beta", np.tile(beta, G))
    for name, v in (("gn_eps", GN_EPS), ("bn_eps", BN_EPS), ("root", -0.5), ("minus", -1.0)):
        put(name, np.full(P, v))
    return t


def kernel(x, L0_conv_w1, L0_conv_wg, L0_conv_w2, L1_conv_kernel, L2_conv_W_qk, L2_conv_b_qk, L2_conv_temperature,
           L3_conv_W1, L3_conv_b1, L3_conv_gamma, L3_conv_beta):
    import concourse.bacc as bacc
    from concourse.bass_utils import run_bass_kernel_spmd

    weights = [np.asarray(a) for a in (
        L0_conv_w1, L0_conv_wg, L0_conv_w2, L1_conv_kernel, L2_conv_W_qk, L2_conv_b_qk, L2_conv_temperature,
        L3_conv_W1, L3_conv_b1, L3_conv_gamma, L3_conv_beta)]
    choose = np.zeros((W // 4, G, W // 4, G, C), np.float32)
    for w in range(W // 4):
        for g in range(G):
            choose[w, g, w, g] = 1
    arrays = {"x": np.ascontiguousarray(x), "consts": constants(*weights), "choose": choose.reshape(P, W // 4, P)}
    nc = bacc.Bacc("TRN2", target_bir_lowering=False, num_devices=1)
    ins = [nc.dram_tensor(k, a.shape, mybir.dt.float32, kind="ExternalInput").ap() for k, a in arrays.items()]
    out = nc.dram_tensor("out", (B, H, W, C), mybir.dt.float32, kind="ExternalOutput").ap()
    build(nc, *ins, out)
    return run_bass_kernel_spmd(nc, [arrays], core_ids=[0]).results[0]["out"]
```

```python
import numpy as np
import concourse.bass as bass
from concourse import mybir
from contextlib import ExitStack

P = 128
B, H, W, C = 8, 128, 128, 32
G = P // C
NS = B // G
PIX = W * H
MULTI = 4
HEADS, WS = 4, 8
CK = C // HEADS
NWIN = W // WS
N = WS * WS
TAPS = 4
PW, PH = 16, 8
OW = PW - TAPS + 1
OH = PH + TAPS - 1
STRIPS = -(-W // OW)
LAST_W = W - OW * (STRIPS - 1)
QUARTERS, QP = 4, 4
QH = QP * PH
PAIRS = QUARTERS * QP // 2
SPANS = {3: (0, 32), 4: (32, 48), 5: (48, 64), 6: (64, 80), 7: (80, 96), 8: (96, 128)}
COLS = 96
K9 = 9
BANK = 512
NB = PIX // BANK
CHUNK = 4 * BANK
RING, DEEP = 2, 4
ROWS = 8
GN_EPS, BN_EPS, LEAKY = 1e-5, 1e-3, 0.3

FIELDS = [
    ("ident", P), ("wg", MULTI * G * C), ("w2", MULTI), ("fir", OW * OH), ("wk", P), ("temp", P), ("bk", P),
    ("wq", HEADS * N), ("bq", N), ("bkc", 1), ("tempc", 1), ("w9", COLS), ("b9", G * K9),
    ("shift", 3 * P), ("mean8", P), ("w1", MULTI), ("gamma", 1), ("beta", 1), ("gn_eps", 1), ("bn_eps", 1),
    ("root", 1), ("minus", 1),
]
AT, _n = {}, 0
for _name, _size in FIELDS:
    AT[_name] = (_n, _size)
    _n += _size
NCONST = _n


def build(nc, x, consts, choose, out):
    fp32 = mybir.dt.float32
    ALU = mybir.AluOpType
    ACT = mybir.ActivationFunctionType
    ds = bass.ds
    ctx = ExitStack()
    with ctx:
        def sb(name, cols):
            return ctx.enter_context(nc.sbuf_tensor(name, [P, cols], fp32))

        def sem(name):
            return ctx.enter_context(nc.semaphore(name))

        X = sb("X", NS * PIX)
        cst = sb("cst", NCONST)
        ST = sb("ST", NS * 4 * H)
        MW = NWIN * NWIN * (C + 1)
        work = sb("work", MW + 7168)
        stats = sb("stats", 64 * 6)
        mv = sb("mv", 2)
        co = sb("co", 4)
        l0s = sb("l0s", 2 * MULTI)
        warm = sb("warm", 2)
        ksum = sb("ksum", NWIN * NWIN)
        vall = sb("vall", 4 * NS)
        bns = sb("bns", 16)
        ps = ctx.enter_context(nc.psum_tensor("ps", [P, 8, BANK], fp32))

        X3 = X[:, :].rearrange("p (w h) -> p w h", h=H)
        X5 = X[:, :].rearrange("p (b w h) -> p b w h", w=W // 4, h=H)
        X4 = X[:, :].rearrange("p (j w h) -> p j w h", w=NWIN, h=H)

        def c(name, rows=slice(0, P)):
            a, n = AT[name]
            return cst[rows, a:a + n]

        ident = c("ident")
        wg = c("wg").rearrange("p (m n) -> p m n", m=MULTI)
        wq = c("wq").rearrange("p (h n) -> p h n", h=HEADS)
        shift = c("shift").rearrange("p (k n) -> p k n", k=3)
        rstd, nmr, minus_mean = co[:, 0:1], co[:, 1:2], co[:, 2:3]
        ve = co[:, 3:4]

        def columns(s, w):
            return X5[:, ds(s * 4, 4), ds(w, 1), :].rearrange("p b o h -> p (b o) h")

        def rows4(v):
            return v.rearrange("p (b h) -> p b h", b=4)

        def part(at, shape):
            n = int(np.prod(shape))
            v = work[:, at:at + n]
            names = "abcdef"[:len(shape)]
            pat = "p (" + " ".join(names) + ") -> p " + " ".join(names)
            return v.rearrange(pat, **{k: s for k, s in zip(names[1:], shape[1:])}), at + n

        LOADS, LW = 4, 8
        stage, _e = part(0, [LOADS, G, LW * C])
        lined, _ = part(_e, [RING, LW, G, C])
        yb, _e = part(0, [DEEP, CHUNK])
        zb, _e = part(_e, [RING, CHUNK])
        acc, _ = part(_e, [CHUNK])
        strip, _e = part(0, [DEEP, H, PW])
        patch, _ = part(_e, [DEEP, QP, P])
        mall, _e0 = part(0, [NWIN, NWIN, C + 1])
        xn, _e = part(_e0, [RING, NWIN, WS, WS])
        xw, _e = part(_e, [RING, 4, P])
        kh, _e = part(_e, [RING, 4, G, P])
        mh, _e = part(_e0, [RING, NWIN, G, C])
        assert NWIN * G * C == RING * NWIN * WS * WS
        rs, _e = part(_e, [RING, 4, P])
        qb, _ = part(_e, [RING, NWIN // 2, WS, WS])
        T, _e = part(0, [W + 2, G * K9])
        xc, _e = part(_e, [DEEP, BANK])
        s_rows, _e = part(_e, [W * G])
        sel, _e = part(_e, [W // 4, P])
        vb, _v = part(_e, [DEEP, BANK])
        xd, _ = part(_v, [RING, BANK])
        U, _ = part(_v, [3, W, G])
        row, _o = part(0, [ROWS, BANK])
        assert _o <= (W + 2) * G * K9 and LOADS * G * LW * C <= (W + 2) * G * K9 + DEEP * BANK
        ob, _ = part(_e, [RING, G, 4, 4, C])

        ring_sems = {}

        def rsem(name, owner, ring=RING):
            s = sem(name)
            ring_sems.setdefault(owner, []).append((s, ring))
            return s

        def after(n, ring=RING):
            return n + 1 + ring

        def slot(n):
            return n + 1

        s_const = sem("consts_loaded")
        s_ident = sem("ident_loaded")
        s_warm = sem("warm_set")
        s_stage = sem("stage_ended")
        s_passed = sem("wait_passed")
        s_load = [sem(f"chunk_loaded{u}") for u in range(LOADS)]
        s_lined = sem("chunk_lined_up")
        s_in = sem("bank_transposed")
        s_inst = sem("bank_measured")
        s_bank = sem("bank_copied")
        s_aggr = sem("moments_ready")
        s_pool = sem("pool_step")
        s_y = sem("y_ready")
        s_zp = sem("z_projected")
        s_zs = rsem("z_ready", "act")
        s_x1 = rsem("z_added", "dve")
        s_strip = sem("strip_ready")
        s_next = rsem("next_strip_ready", "pool")
        s_zero = sem("keys_buffers_zeroed")
        s_mz = sem("m_buffer_zeroed")
        s_pt = sem("patches_transposed")
        s_pc = rsem("patches_copied", "act", DEEP)
        s_cv = rsem("pair_filtered", "pe", 2 * DEEP)
        s_x2 = rsem("pair_added", "dve", 2 * RING)
        s_xn = sem("windows_normalised")
        s_wt = sem("windows_projected")
        s_xw = rsem("xw_ready", "act")
        s_kh = rsem("kh_ready", "dve")
        s_m = rsem("m_summed", "pe")
        s_mc = rsem("m_copied", "act")
        s_sp = sem("sums_projected")
        s_qb = sem("query_bias_ready")
        s_xb = rsem("query_bias_added", "dve", 1)
        s_xg = rsem("query_bias_added_second", "pool", 1)
        s_mh = sem("mh_ready")
        s_r = sem("r_summed")
        s_rc = rsem("r_copied", "act")
        s_xt = rsem("r_transposed", "pe")
        s_x3 = rsem("x3_written", "dve")
        s_xc = sem("x3n_ready")
        s_tp = rsem("t_projected", "pe", DEEP)
        s_td = rsem("t_stored", "dve", DEEP)
        s_sm = sem("s_summed")
        s_ss = sem("s_stored")
        s_u = sem("w_summed")
        s_sel = sem("sel_loaded")
        s_sc = sem("s_spread")
        s_v = [rsem("even_v_ready", "dve"), rsem("odd_v_ready", "pool")]
        s_so = rsem("odd_s_copied", "act")
        s_vm = rsem("odd_v_measured", "dve")
        s_g = sem("bn_step")
        s_fc = sem("out_s_spread")
        s_fv = rsem("out_v_ready", "dve", DEEP)
        s_fy = sem("out_y_ready")
        s_fl = sem("out_l_ready")
        s_fo = sem("out_sum_ready")
        s_ft = rsem("out_transposed", "pe", ROWS)
        s_fe = rsem("out_chunk_ready", "act", DEEP)
        s_out = [sem(f"chunk_stored{u}") for u in range(RING)]

        STAGES = 8
        UNITS = PIX // CHUNK * MULTI
        ENG = 5

        def alone(eng):
            eng.sem_inc(s_passed, 1)

        def stage_end(eng, s, k):
            eng.drain().then_inc(s_stage, 1)
            eng.wait_ge(s_stage, s * (STAGES * ENG) + (k + 1) * ENG)
            alone(eng)

        def start_rings(eng, owner):
            for s, ring in ring_sems.get(owner, []):
                eng.sem_inc(s, ring)

        def spread_s(s, n, bank):
            return nc.tensor.matmul(ps[:, bank, :], sel[:, n, :], ST[:, ds(s * (4 * H), 4 * H)], start=True, stop=True)

        def norm_strip(eng, done, s, t, u, lo, hi):
            eng.tensor_scalar(strip[:, u, :, lo:hi].rearrange("p h w -> p w h"),
                              X3[:, ds(s * W + t * OW + (lo - 1), hi - lo), :], rstd, nmr,
                              ALU.mult, ALU.add).then_inc(done, 1)

        block = ctx.enter_context(nc.Block())

        @block.sync
        def _(sp):
            def load(s, n, u):
                sp.dma_start(stage[:, u, :, :],
                             x[s * G:s * G + G, :, ds(n * LW, LW), :].rearrange("g h w c -> h g (w c)")
                             ).then_inc(s_load[u], 16)

            sp.dma_start(ident, consts[:, 0:P]).then_inc(s_ident, 16)
            for u in range(LOADS):
                load(0, u, u)
            sp.dma_start(cst[:, P:NCONST], consts[:, P:NCONST]).then_inc(s_const, 16)
            for s in range(NS):
                with sp.Fori(1, W // LW // LOADS) as i:
                    for u in range(LOADS):
                        sp.wait_ge(s_lined, i * 4 + (s * 16 + u - 3))
                        alone(sp)
                        load(s, i * LOADS + u, u)
                for k in range(STAGES):
                    if k == 5:
                        sp.dma_start(sel[:, :, :], choose[:, :, :]).then_inc(s_sel, 16)
                    if k == 7 and s + 1 < NS:
                        for u in range(LOADS):
                            load(s + 1, u, u)
                    sp.drain().then_inc(s_stage, 1)
                    sp.wait_ge(s_stage, s * (STAGES * ENG) + (k + 1) * ENG)
            with sp.Fori(0, NS) as s:
                with sp.Fori(0, 4) as i:
                    for u in range(RING):
                        sp.wait_ge(s_fe, after(s * NB + i * 8 + (4 * u + 3), DEEP))
                        for g in range(G):
                            o = out.rearrange("i h (b w) c -> h i b (w c)", b=4)
                            o = o[:, ds(s * G + g, 1), :, ds(i * (8 * C) + 4 * C * u, 4 * C)]
                            sp.dma_start(o.rearrange("h a b w -> h (a b) w"),
                                         ob[:, u, g, :, :, :].rearrange("p b w c -> p b (w c)")).then_inc(s_out[u], 16)
            for u in range(RING):
                sp.wait_ge(s_out[u], NS * 4 * 64 + 64)

        @block.tensor
        def _(pe):
            start_rings(pe, "pe")
            pe.sem_inc(s_in, 2 * RING)
            pe.sem_inc(s_r, 2 * RING)
            pe.wait_ge(s_ident, 16)
            with pe.Fori(0, NS) as s:
                with pe.Fori(0, W // LW // LOADS) as i:
                    for u in range(LOADS):
                        pe.wait_ge(s_lined, s * 16 + i * 4 + (u + 1))
                        for b in range(2):
                            pe.wait_ge(s_bank, s * NB + i * 8 + (2 * u + b + 1))
                            for w in range(4):
                                one_w = lined[:, u % 2, 4 * b + w, :, :].rearrange("p g c -> p (g c)")
                                last = pe.transpose(ps[:, 2 * u + b, w * H:(w + 1) * H], one_w, ident)
                            last.then_inc(s_in, 1)
                stage_end(pe, s, 0)

                with pe.Fori(0, PIX // CHUNK) as i:
                    for m in range(MULTI):
                        k = s * UNITS + i * MULTI + m
                        pe.wait_ge(s_y, k + 1)
                        pe.wait_ge(s_zs, slot(k))
                        for b in range(4):
                            last = pe.matmul(ps[:, 4 * (m % 2) + b, :], wg[:, m, :], yb[:, m, b * BANK:(b + 1) * BANK],
                                             start=True, stop=True)
                        last.then_inc(s_zp, 1)
                stage_end(pe, s, 1)

                def to_patches(t, u, q):
                    nn = (s * STRIPS + t) * QUARTERS + q
                    if q == 0:
                        pe.wait_ge(s_next, s * (STRIPS - 2) + t + 1)
                        if u == 1:
                            pe.wait_ge(s_strip, s * 3 + 3)
                    if u == 0 and q == 1:
                        pe.wait_ge(s_strip, s * 3 + 2)
                    pe.wait_ge(s_pc, slot(nn))
                    for k in range(QP):
                        rows = strip[:, u, q * QH + k * PH:q * QH + (k + 1) * PH, :]
                        last = pe.transpose(ps[:, q, k * P:k * P + P], rows.rearrange("p h w -> p (h w)"), ident)
                    last.then_inc(s_pt, 1)

                def filtered(t, q):
                    nn = (s * STRIPS + t) * QUARTERS + q
                    pe.wait_ge(s_pc, after(nn, DEEP))
                    for par in range(2):
                        pe.wait_ge(s_x2, slot(nn * 2 + par))
                        for k in range(par, QP, 2):
                            at = k // 2 * (OW * OH)
                            last = pe.matmul(ps[:, DEEP + 2 * (q % 2) + par, at:at + OW * OH],
                                             patch[:, q, k, :], c("fir"), start=True, stop=True)
                        last.then_inc(s_cv, 1)

                def strips(t, n, last=False):
                    for u in range(n):
                        for q in range(QUARTERS):
                            t1, q1 = u + (q + 1) // QUARTERS, (q + 1) % QUARTERS
                            if not (last and t1 == n):
                                to_patches(t + t1, t1 % DEEP, q1)
                            filtered(t + u, q)

                pe.wait_ge(s_strip, s * 3 + 1)
                to_patches(0, 0, 0)
                with pe.Fori(0, STRIPS // DEEP) as i:
                    strips(i * DEEP, DEEP)
                strips(STRIPS // DEEP * DEEP, STRIPS % DEEP, last=True)
                stage_end(pe, s, 2)

                def project(w1, n, xu, hf):
                    nn = s * NB + n
                    if hf == 0:
                        pe.wait_ge(s_xn, s * NWIN + w1 + 1)
                    pe.wait_ge(s_xw, slot(nn))
                    pe.wait_ge(s_kh, slot(nn))
                    for what, bank in ((ident, 0), (c("wk"), 2)):
                        for pp in range(4):
                            h1 = 2 * (4 * hf + pp)
                            px = xn[:, xu, h1:h1 + 2, :, :].rearrange("p h j i -> p (h j i)")
                            o = ps[:, bank + hf, pp * P:pp * P + P]
                            if bank == 0:
                                pe.transpose(o, px, what)
                            else:
                                last = pe.matmul(o, px, what, start=True, stop=True)
                    last.then_inc(s_wt, 1)

                def m_sum(n, u):
                    nn = s * NB + n
                    pe.wait_ge(s_xw, after(nn))
                    pe.wait_ge(s_kh, after(nn))
                    pe.wait_ge(s_mc, slot(nn))
                    for pp in range(4):
                        for g in range(G):
                            last = pe.matmul(ps[C * g:C * g + C, 4 + u, pp * P:pp * P + P],
                                             xw[:, u, pp, C * g:C * g + C], kh[:, u, pp, g, :],
                                             start=True, stop=True)
                    last.then_inc(s_m, 1)

                project(0, 0, 0, 0)
                project(0, 1, 0, 1)
                m_sum(0, 0)
                with pe.Fori(0, 7) as i:
                    for u in range(2):
                        w1 = i * 2 + (u + 1)
                        project(w1, w1 * 2, 1 - u, 0)
                        m_sum(w1 * 2 - 1, 1)
                        project(w1, w1 * 2 + 1, 1 - u, 1)
                        m_sum(w1 * 2, 0)
                project(NWIN - 1, NB - 2, 1, 0)
                m_sum(NB - 3, 1)
                project(NWIN - 1, NB - 1, 1, 1)
                m_sum(NB - 2, 0)
                m_sum(NB - 1, 1)
                pe.wait_ge(s_mc, after(s * NB + NB - 1))
                pe.matmul(ps[:, 6, 0:NWIN * NWIN], c("wk"), mall[:, :, :, C:C + 1].rearrange("p a b o -> p (a b o)"),
                          start=True, stop=True).then_inc(s_sp, 1)
                stage_end(pe, s, 3)

                def r_sum(w1, n, mu, hf):
                    nn = s * NB + n
                    if hf == 0:
                        pe.wait_ge(s_mh, s * NWIN + w1 + 1)
                    pe.wait_ge(s_rc, slot(nn))
                    for hp in range(2):
                        for hd in range(HEADS):
                            mvg = mh[:, mu, 8 * hf + hp:8 * hf + hp + 7:2, :, hd * CK:hd * CK + CK]
                            o = ps[N * hp:N * hp + N, hf, :].rearrange("p (q g d) -> p q g d", q=4, g=G)
                            last = pe.matmul(o[:, :, :, hd * CK:hd * CK + CK], wq[:, hd, :], mvg,
                                             start=(hd == 0), stop=(hd == HEADS - 1))
                    last.then_inc(s_r, 1)

                def r_back(n, u):
                    nn = s * NB + n
                    pe.wait_ge(s_rc, after(nn))
                    pe.wait_ge(s_x3, slot(nn))
                    for q in range(4):
                        last = pe.transpose(ps[:, 2 + u, q * P:q * P + P], rs[:, u, q, :], ident)
                    last.then_inc(s_xt, 1)

                r_sum(0, 0, 0, 0)
                r_sum(0, 1, 0, 1)
                r_back(0, 0)
                with pe.Fori(0, 7) as i:
                    for u in range(2):
                        w1 = i * 2 + (u + 1)
                        r_sum(w1, w1 * 2, 1 - u, 0)
                        r_back(w1 * 2 - 1, 1)
                        r_sum(w1, w1 * 2 + 1, 1 - u, 1)
                        r_back(w1 * 2, 0)
                r_sum(NWIN - 1, NB - 2, 1, 0)
                r_back(NB - 3, 1)
                r_sum(NWIN - 1, NB - 1, 1, 1)
                r_back(NB - 2, 0)
                r_back(NB - 1, 1)
                stage_end(pe, s, 4)

                with pe.Fori(0, 8) as i:
                    for u in range(DEEP):
                        nn = s * NB + i * DEEP + u
                        pe.wait_ge(s_xc, nn + 1)
                        pe.wait_ge(s_td, slot(nn))
                        for w in range(4):
                            last = pe.matmul(ps[:, u, w * COLS:w * COLS + COLS], xc[:, u, w * H:w * H + H], c("w9"),
                                             start=True, stop=True)
                        last.then_inc(s_tp, 1)
                stage_end(pe, s, 5)
                for ki in range(3):
                    pe.wait_ge(s_u, s * 6 + 2 * ki + 2)
                    last = pe.matmul(ps[:, 7, :], shift[:, ki, :], U[:, ki, :, :].rearrange("p w g -> p (w g)"),
                                     start=(ki == 0), stop=(ki == 2))
                last.then_inc(s_sm, 1)
                pe.wait_ge(s_ss, s + 1)
                for b in range(4):
                    last = pe.transpose(ps[:, 6, b * H:b * H + H], s_rows[:, b * P:b * P + P], ident)
                last.then_inc(s_sm, 1)
                stage_end(pe, s, 6)
                pe.wait_ge(s_sel, s * 16 + 16)
                for n in range(NB):
                    pe.wait_ge(s_so if n % 2 else s_v[0], slot(s * (NB // 2) + n // 2))
                    spread_s(s, n, n % DEEP).then_inc(s_sc, 1)
                stage_end(pe, s, 7)
            pe.wait_ge(s_g, 2)
            pe.matmul(ps[:, DEEP, 0:NS], c("mean8"), bns[:, 0:2], start=True, stop=True).then_inc(s_g, 1)
            pe.wait_ge(s_g, 7)
            pe.matmul(ps[:, DEEP + 1, 0:NS], c("mean8"), bns[:, 4:6], start=True, stop=True).then_inc(s_g, 1)
            with pe.Fori(0, NS) as s:
                def out_s(n):
                    pe.wait_ge(s_fv, slot(s * NB + n))
                    spread_s(s, n, n % DEEP).then_inc(s_fc, 1)

                def out_t(n):
                    nn = s * NB + n
                    pe.wait_ge(s_fo, nn + 1)
                    pe.wait_ge(s_fe, slot(nn))
                    for w in range(4):
                        last = pe.transpose(ps[:, DEEP + n % DEEP, w * P:w * P + P], row[:, n % ROWS, w * H:w * H + H],
                                            ident)
                    last.then_inc(s_ft, 1)

                for n in range(DEEP + 1):
                    out_s(n)
                for n in range(NB):
                    if n + DEEP + 1 < NB:
                        out_s(n + DEEP + 1)
                    out_t(n)

        @block.scalar
        def _(act):
            start_rings(act, "act")
            act.sem_inc(s_bank, 8)
            act.wait_ge(s_warm, 1)
            act.sem_inc(s_out[0], 64)
            act.sem_inc(s_out[1], 64)
            with act.Fori(0, NS) as s:
                with act.Fori(0, 4) as i:
                    for b in range(8):
                        act.wait_ge(s_inst, s * NB + i * 8 + b + 1)
                        act.activation(X[:, ds(s * PIX + i * 8 * BANK + b * BANK, BANK)], ps[:, b, :], ACT.Copy
                                       ).then_inc(s_bank, 1)
                act.activation(warm[:, 1:2], warm[:, 0:1], ACT.Gelu)
                stage_end(act, s, 0)

                def gelu_y(i, m):
                    act.activation(yb[:, m, :], X[:, ds(s * PIX + i * CHUNK, CHUNK)], ACT.Gelu,
                                   scale=l0s[:, m:m + 1], bias=l0s[:, MULTI + m:MULTI + m + 1]).then_inc(s_y, 1)

                def gelu_z(i, m):
                    k = s * UNITS + i * MULTI + m
                    act.wait_ge(s_zp, k + 1)
                    act.wait_ge(s_x1, slot(k))
                    act.activation(zb[:, m % 2, :], ps[:, 4 * (m % 2):4 * (m % 2) + 4, :].rearrange("p a b -> p (a b)"),
                                   ACT.Gelu).then_inc(s_zs, 1)

                gelu_y(0, 0)
                gelu_y(0, 1)
                with act.Fori(0, PIX // CHUNK - 1) as i:
                    for m in range(MULTI):
                        gelu_y(i + (m + 2) // MULTI, (m + 2) % MULTI)
                        gelu_z(i, m)
                for m in range(MULTI):
                    if m + 2 < MULTI:
                        gelu_y(PIX // CHUNK - 1, m + 2)
                    gelu_z(PIX // CHUNK - 1, m)
                stage_end(act, s, 1)

                with act.Fori(0, STRIPS // 2) as i:
                    for w in range(2 * QUARTERS):
                        q = w % QUARTERS
                        nn = (s * STRIPS + i * 2) * QUARTERS + w
                        act.wait_ge(s_pt, nn + 1)
                        act.wait_ge(s_cv, slot(nn * 2 + 1))
                        act.activation(patch[:, q, :, :].rearrange("p a b -> p (a b)"), ps[:, q, :], ACT.Copy
                                       ).then_inc(s_pc, 1)
                stage_end(act, s, 2)

                def copy_xw(n, u):
                    nn = s * NB + n
                    act.wait_ge(s_wt, nn + 1)
                    act.wait_ge(s_m, slot(nn))
                    act.activation(xw[:, u, :, :].rearrange("p a b -> p (a b)"), ps[:, u, :], ACT.Copy
                                   ).then_inc(s_xw, 1)

                def copy_m(n, u):
                    nn = s * NB + n
                    act.wait_ge(s_m, after(nn))
                    src = ps[:, 4 + u, :].rearrange("p (a b) -> p a b", b=N)[:, :, 0:C + 1]
                    dst = work[:, ds(n * (8 * (C + 1)), 8 * (C + 1))].rearrange("p (a b) -> p a b", b=C + 1)
                    act.activation(dst, src, ACT.Copy).then_inc(s_mc, 1)

                copy_xw(0, 0)
                with act.Fori(0, 15) as i:
                    for u in range(2):
                        copy_xw(i * 2 + (u + 1), 1 - u)
                        copy_m(i * 2 + u, u)
                copy_xw(NB - 1, 1)
                copy_m(NB - 2, 0)
                copy_m(NB - 1, 1)
                stage_end(act, s, 3)

                def spread_m(w1, u):
                    act.wait_ge(s_r, s * NB + w1 * 2 + 2)
                    for g in range(G):
                        src = work[C * g:C * g + C, ds(w1 * (NWIN * (C + 1)), NWIN * (C + 1))
                                   ].rearrange("p (a b) -> p a b", b=C + 1)[:, :, 0:C]
                        last = act.activation(mh[C * g:C * g + C, u, :, g, :], src, ACT.Copy)
                    last.then_inc(s_mh, 1)

                def copy_r(n, u):
                    nn = s * NB + n
                    act.wait_ge(s_r, after(nn) + RING)
                    act.wait_ge(s_xt, slot(nn))
                    act.activation(rs[:, u, :, :].rearrange("p a b -> p (a b)"), ps[:, u, :], ACT.Copy
                                   ).then_inc(s_rc, 1)

                act.wait_ge(s_mz, s * RING + 1)
                spread_m(0, 0)
                act.wait_ge(s_mz, s * RING + 2)
                with act.Fori(0, 7) as i:
                    for u in range(2):
                        w1 = i * 2 + u
                        spread_m(w1 + 1, 1 - u)
                        copy_r(w1 * 2, 0)
                        copy_r(w1 * 2 + 1, 1)
                spread_m(NWIN - 1, 1)
                for n in range(NB - 4, NB):
                    copy_r(n, n % 2)
                stage_end(act, s, 4)

                with act.Fori(0, 8) as i:
                    for u in range(DEEP):
                        nn = s * NB + i * DEEP + u
                        act.wait_ge(s_tp, slot(nn))
                        x_in = X[:, ds(s * PIX + i * (DEEP * BANK) + u * BANK, BANK)]
                        act.activation(xc[:, u, :], x_in, ACT.Identity,
                                       scale=rstd, bias=nmr).then_inc(s_xc, 1)
                stage_end(act, s, 5)
                stage_end(act, s, 6)
                with act.Fori(0, 8) as i:
                    for u in range(1, DEEP, 2):
                        nn = s * (NB // 2) + i * 2 + u // 2
                        act.wait_ge(s_sc, s * NB + i * DEEP + (u + 1))
                        act.wait_ge(s_vm, slot(nn))
                        act.activation(rows4(xd[:, u // 2, :]), columns(s, i * DEEP + u), ACT.Identity, bias=minus_mean)
                        act.activation(vb[:, u, :], ps[:, u, :], ACT.Copy).then_inc(s_so, 1)
                stage_end(act, s, 7)
            for s in range(NS):
                def norm(n, u):
                    act.wait_ge(s_fv, after(s * NB + n, DEEP))
                    act.activation(row[:, u, :], row[:, u, :], ACT.Identity, scale=bns[:, 12 + s:13 + s],
                                   bias=bns[:, 15:16]).then_inc(s_fy, 1)

                def lay(n, j, k, i):
                    act.wait_ge(s_ft, after(s * NB + n, ROWS))
                    if j == 0:
                        act.wait_ge(s_out[k], s * 256 + i * 64 + 64)
                    o = ob[:, k, :, :, j, :].rearrange("p g b c -> p b g c")
                    act.activation(o, ps[:, DEEP + j, :].rearrange("p (b g c) -> p b g c", b=4, g=G), ACT.Copy
                                   ).then_inc(s_fe, 1)

                LEAD = 4
                for n in range(LEAD):
                    norm(n, n)
                with act.Fori(0, 3) as i:
                    for j in range(8):
                        norm(i * 8 + (j + LEAD), (j + LEAD) % ROWS)
                        lay(i * 8 + j, j % 4, j // 4, i)
                for j in range(8):
                    if j + LEAD < 8:
                        norm(24 + j + LEAD, j + LEAD)
                    lay(24 + j, j % 4, j // 4, 3)

        @block.vector
        def _(dve):
            start_rings(dve, "dve")
            with dve.Fori(0, NS) as s:
                def measure(i, u):
                    for b in range(2 * u, 2 * u + 2):
                        dve.wait_ge(s_in, after(s * NB + i * 8 + b) + RING)
                        dve.bn_stats(stats[:, ds(i * 48 + 6 * b, 6)], ps[:, b, :]).then_inc(s_inst, 1)

                def moments(n):
                    dve.drain()
                    dve.bn_aggr(mv[:, :], stats[:, 0:6 * n]).then_inc(s_aggr, 1)

                with dve.Fori(0, 4) as i:
                    for u in range(LOADS):
                        dve.wait_ge(s_load[u], s * 64 + i * 16 + 16)
                        dve.wait_ge(s_in, s * NB + i * 8 + (2 * u + 2))
                        dve.tensor_copy(lined[:, u % 2, :, :, :],
                                        stage[:, u, :, :].rearrange("p g (w c) -> p w g c", c=C)).then_inc(s_lined, 1)
                        if u:
                            measure(i, u - 1)
                    measure(i, LOADS - 1)
                moments(NB)
                stage_end(dve, s, 0)

                with dve.Fori(0, PIX // CHUNK) as i:
                    x_in = X[:, ds(s * PIX + i * CHUNK, CHUNK)]
                    for m in range(MULTI):
                        k = s * UNITS + i * MULTI + m
                        dve.wait_ge(s_zs, after(k))
                        dve.wait_ge(s_x1, slot(k) + 1)
                        dve.scalar_tensor_tensor(acc if m < MULTI - 1 else x_in, zb[:, m % 2, :],
                                                 c("w2")[:, m:m + 1], acc if m else x_in, ALU.mult, ALU.add
                                                 ).then_inc(s_x1, 1)
                    dve.wait_ge(s_x1, after(k))
                    alone(dve)
                    for b in range(4):
                        dve.bn_stats(stats[:, ds(i * 24 + 6 * b, 6)], X[:, ds(s * PIX + i * CHUNK + b * BANK, BANK)])
                moments(NB)
                stage_end(dve, s, 1)

                def add_pair(t, j, ow):
                    nn = (s * STRIPS + t) * PAIRS + j
                    q, par = j // 2, j % 2
                    dve.wait_ge(s_cv, after(nn, 2 * DEEP))
                    dve.wait_ge(s_x2, after(nn - 1, 2 * RING))
                    src = ps[:, DEEP + 2 * (q % 2) + par, 0:2 * OW * OH].rearrange("p (k w h) -> p w k h", k=2, h=OH)
                    top = q * QH + par * PH - 2
                    if top >= 0 and top + 4 * PH <= H:
                        v = X3[:, ds(s * W + t * OW, ow), top:top + 4 * PH]
                        v = v.rearrange("p w (k h) -> p w k h", k=2)[:, :, :, 0:OH]
                        last = dve.tensor_tensor(v, v, src[:, 0:ow], ALU.add)
                    else:
                        for k in range(2):
                            h0 = top + k * 2 * PH
                            lo, n = max(0, -h0), min(OH, H - h0)
                            v = X3[:, ds(s * W + t * OW, ow), h0 + lo:h0 + n]
                            last = dve.tensor_tensor(v, v, src[:, 0:ow, k, lo:n], ALU.add)
                    last.then_inc(s_x2, 1)

                def measure_x2(t, j, ow):
                    lo, hi = SPANS[j]
                    dve.wait_ge(s_x2, after((s * STRIPS + t) * PAIRS + j - 1, 2 * RING))
                    alone(dve)
                    dve.bn_stats(stats[:, ds(t * (6 * len(SPANS)) + 6 * (j - 3), 6)],
                                 X3[:, ds(s * W + t * OW, ow), lo:hi])

                def add_strip(t, ow):
                    dve.wait_ge(s_next, s * (STRIPS - 2) + t + (2 if ow == OW else 1))
                    for j in range(PAIRS):
                        add_pair(t, j, ow)
                        if j in SPANS:
                            measure_x2(t, j, ow)
                    measure_x2(t, PAIRS, ow)

                dve.memset(strip[:, 0, :, 0:1], 0.0)
                for rows in (slice(0, QH), slice(QH, H)):
                    dve.tensor_scalar(strip[:, 0, rows, 1:PW].rearrange("p h w -> p w h"),
                                      X3[:, ds(s * W, PW - 1), rows], rstd, nmr, ALU.mult, ALU.add).then_inc(s_strip, 1)
                norm_strip(dve, s_strip, s, 1, 1, 0, PW)
                dve.wait_ge(s_strip, s * 3 + 3)
                alone(dve)
                with dve.Fori(0, STRIPS // 3) as i:
                    for u in range(3):
                        add_strip(i * 3 + u, OW)
                add_strip(STRIPS - 1, LAST_W)
                moments(STRIPS * len(SPANS))
                stage_end(dve, s, 2)

                def norm_windows(w1, u):
                    dve.tensor_scalar(xn[:, u, :, :, :].rearrange("p h j i -> p j i h"),
                                      X4[:, ds(s * 8, 8), ds(w1, 1), :].rearrange("p j a (i h) -> p (j a) i h", i=WS),
                                      rstd, nmr, ALU.mult, ALU.add).then_inc(s_xn, 1)

                def keys(n, u):
                    nn = s * NB + n
                    dve.wait_ge(s_wt, nn + 1)
                    dve.wait_ge(s_m, slot(nn))
                    for hp in range(2):
                        rows = slice(N * hp, N * hp + N)
                        k_in = ps[rows, 2 + u, :].rearrange("p (a g d) -> p a g d", a=4, g=G)
                        bias = c("bk", rows).rearrange("p (o g d) -> p o g d", o=1, g=G).broadcast_to([N, 4, G, C])
                        o = kh[rows, u, :, :, N * hp:N * hp + C]
                        last = dve.tensor_tensor(o, k_in, bias, ALU.add)
                    last.then_inc(s_kh, 1)

                dve.wait_ge(s_zero, s + 1)
                norm_windows(0, 0)
                norm_windows(1, 1)
                with dve.Fori(0, 7) as i:
                    for u in range(2):
                        w1 = i * 2 + u
                        keys(w1 * 2, 0)
                        keys(w1 * 2 + 1, 1)
                        norm_windows(w1 + 2, u)
                for n in range(NB - 4, NB):
                    keys(n, n % 2)
                dve.memset(mh[:, 0, :, :, :], 0.0).then_inc(s_mz, 1)
                dve.wait_ge(s_sp, s + 1)
                dve.scalar_tensor_tensor(ksum[:, :], c("bkc").broadcast_to([P, NWIN * NWIN]), float(N),
                                         ps[:, 6, 0:NWIN * NWIN], ALU.mult, ALU.add)
                stage_end(dve, s, 3)

                dve.memset(mh[:, 1, :, :, :], 0.0).then_inc(s_mz, 1)
                with dve.Fori(0, 16) as i:
                    def half_windows(hf):
                        return X3[:, ds(s * W + i * WS, WS), 64 * hf:64 * hf + 64]

                    def measure_x3(hf):
                        dve.wait_ge(s_x3, after(s * NB + i * 2 + hf))
                        alone(dve)
                        dve.bn_stats(stats[:, ds(i * 12 + 6 * hf, 6)], half_windows(hf))

                    def windows(hf):
                        return half_windows(hf).rearrange("p j (q i) -> p j q i", i=WS)

                    dve.wait_ge(s_qb, s * NB + i * 2 + 1)
                    dve.tensor_tensor(windows(0), windows(0), qb[:, 0, :, :, :].rearrange("p q j i -> p j q i"),
                                      ALU.add).then_inc(s_xb, 1)
                    for hf in range(2):
                        nn = s * NB + i * 2 + hf
                        dve.wait_ge(s_xt, after(nn))
                        dve.wait_ge(s_xg if hf else s_xb, after(s * NWIN + i, 1))
                        src = ps[:, 2 + hf, :].rearrange("p (q j i) -> p j q i", j=WS, i=WS)
                        dve.tensor_tensor(windows(hf), windows(hf), src, ALU.add).then_inc(s_x3, 1)
                    measure_x3(0)
                    measure_x3(1)
                moments(NB)
                stage_end(dve, s, 4)

                with dve.Fori(0, 8) as i:
                    for u in range(DEEP):
                        nn = s * NB + i * DEEP + u
                        dve.wait_ge(s_tp, after(nn, DEEP))
                        o = T[:, ds(i * (4 * DEEP) + 4 * u + 1, 4), :]
                        bias = c("b9").rearrange("p (o n) -> p o n", o=1).broadcast_to([P, 4, G * K9])
                        src = ps[:, u, 0:4 * COLS].rearrange("p (w n) -> p w n", n=COLS)[:, :, 0:G * K9]
                        dve.tensor_tensor(o, src, bias, ALU.add).then_inc(s_td, 1)
                dve.drain()
                dve.memset(T[:, 0:2, :], 0.0)
                dve.memset(T[:, W:W + 2, :], 0.0)
                stage_end(dve, s, 5)
                def weight(ki, kj):
                    return T[:, 2 - kj:2 - kj + W, :].rearrange("p w (g k) -> p w g k", k=K9)[:, :, :, 3 * ki + kj]

                for ki in range(3):
                    dve.tensor_tensor(U[:, ki, :, :], weight(ki, 0), weight(ki, 1), ALU.add).then_inc(s_u, 1)
                    dve.wait_ge(s_u, s * 6 + 2 * ki + 1)
                    dve.tensor_tensor(U[:, ki, :, :], U[:, ki, :, :], weight(ki, 2), ALU.add).then_inc(s_u, 1)
                dve.wait_ge(s_sm, s * 2 + 1)
                dve.tensor_copy(s_rows[:, :], ps[:, 7, :]).then_inc(s_ss, 1)
                dve.wait_ge(s_sm, s * 2 + 2)
                dve.tensor_copy(ST[:, ds(s * (4 * H), 4 * H)], ps[:, 6, :])
                stage_end(dve, s, 6)
                with dve.Fori(0, 8) as i:
                    def measure_v(u):
                        dve.wait_ge(s_v[u % 2], after(s * (NB // 2) + i * 2 + u // 2))
                        alone(dve)
                        o = dve.bn_stats(stats[:, ds(i * (6 * DEEP) + 6 * u, 6)], vb[:, u, :])
                        if u % 2:
                            o.then_inc(s_vm, 1)

                    for u in range(DEEP):
                        if u % 2 == 0:
                            dve.wait_ge(s_sc, s * NB + i * DEEP + (u + 1))
                            dve.scalar_tensor_tensor(rows4(vb[:, u, :]), columns(s, i * DEEP + u), minus_mean,
                                                     rows4(ps[:, u, :]), ALU.add, ALU.mult).then_inc(s_v[0], 1)
                        if u:
                            measure_v(u - 1)
                    measure_v(DEEP - 1)
                moments(NB)
                dve.wait_ge(s_aggr, s * 5 + 5)
                alone(dve)
                dve.tensor_copy(vall[:, ds(s * 4, 2)], mv[:, :])
                dve.tensor_copy(vall[:, ds(s * 4 + 2, 1)], rstd)
                dve.tensor_copy(vall[:, ds(s * 4 + 3, 1)], minus_mean)
                stage_end(dve, s, 7)
            dve.wait_ge(s_g, 3)
            va = vall[:, :].rearrange("p (s k) -> p k s", k=4)
            steps = [3]

            def step(ins):
                ins.then_inc(s_g, 1)
                steps[0] += 1
                dve.wait_ge(s_g, steps[0])

            step(dve.tensor_reduce(bns[:, 8:9], ps[:, DEEP, 0:NS], mybir.AxisListType.X, ALU.add))
            step(dve.tensor_scalar(bns[:, 4:6], bns[:, 0:2], bns[:, 8:9], None, ALU.subtract))
            step(dve.tensor_tensor(bns[:, 4:6], bns[:, 4:6], bns[:, 4:6], ALU.mult))
            dve.tensor_tensor(bns[:, 4:6], bns[:, 4:6], bns[:, 2:4], ALU.add).then_inc(s_g, 1)
            dve.wait_ge(s_g, 8)
            steps[0] = 8
            step(dve.tensor_reduce(bns[:, 9:10], ps[:, DEEP + 1, 0:NS], mybir.AxisListType.X, ALU.add))
            dve.wait_ge(s_g, 11)
            steps[0] = 11
            step(dve.tensor_tensor(bns[:, 11:12], bns[:, 10:11], c("gamma"), ALU.mult))
            step(dve.tensor_tensor(bns[:, 12:14], va[:, 2, :], bns[:, 11:12].broadcast_to([P, 2]), ALU.mult))
            step(dve.tensor_tensor(bns[:, 14:15], bns[:, 8:9], bns[:, 11:12], ALU.mult))
            step(dve.tensor_tensor(bns[:, 15:16], c("beta"), bns[:, 14:15], ALU.subtract))
            for s in range(NS):
                def scaled(n, u):
                    dve.wait_ge(s_fc, n + (s * NB + 1))
                    dve.wait_ge(s_ft, slot(n + s * NB))
                    dve.scalar_tensor_tensor(rows4(row[:, u, :]), columns(s, n), vall[:, 4 * s + 3:4 * s + 4],
                                             rows4(ps[:, u % DEEP, :]), ALU.add, ALU.mult).then_inc(s_fv, 1)

                def leaky(n, u):
                    dve.wait_ge(s_fy, n + (s * NB + 1))
                    dve.scalar_tensor_tensor(row[:, u, :], row[:, u, :], LEAKY, row[:, u, :], ALU.mult, ALU.max
                                             ).then_inc(s_fl, 1)

                scaled(0, 0)
                scaled(1, 1)
                with dve.Fori(0, NB // ROWS - 1) as i:
                    for u in range(ROWS):
                        scaled(i * ROWS + (u + 2), (u + 2) % ROWS)
                        leaky(i * ROWS + u, u)
                for n in range(NB - ROWS, NB):
                    if n + 2 < NB:
                        scaled(n + 2, (n + 2) % ROWS)
                    leaky(n, n % ROWS)

        @block.gpsimd
        def _(pool):
            start_rings(pool, "pool")
            pool.memset(warm[:, :], 0.0).then_inc(s_warm, 1)
            pool.wait_ge(s_const, 16)
            pool.tensor_tensor(c("wk"), c("wk"), c("temp"), ALU.mult)
            pool.tensor_tensor(c("bk"), c("bk"), c("temp"), ALU.mult)
            pool.tensor_tensor(c("bkc"), c("bkc"), c("tempc"), ALU.mult)
            PS = 18

            for s in range(NS):
                cnt = [0]

                def step(*ins):
                    cnt[0] += len(ins)
                    for x in ins:
                        x.then_inc(s_pool, 1)
                    pool.wait_ge(s_pool, s * PS + cnt[0])
                    alone(pool)

                def coefficients(k):
                    pool.wait_ge(s_aggr, s * 5 + k + 1)
                    step(pool.tensor_tensor(ve, mv[:, 1:2], c("gn_eps"), ALU.add),
                         pool.tensor_tensor(minus_mean, mv[:, 0:1], c("minus"), ALU.mult))
                    step(pool.tensor_tensor(rstd, ve, c("root"), ALU.pow))
                    step(pool.tensor_tensor(nmr, minus_mean, rstd, ALU.mult))

                coefficients(0)
                step(pool.tensor_tensor(l0s[:, 0:MULTI], c("w1"), rstd.broadcast_to([P, MULTI]), ALU.mult),
                     pool.tensor_tensor(l0s[:, MULTI:2 * MULTI], c("w1"), nmr.broadcast_to([P, MULTI]), ALU.mult))
                stage_end(pool, s, 0)
                coefficients(1)
                stage_end(pool, s, 1)
                pool.memset(kh[:, :, :, :, :], 0.0)
                pool.drain()
                for hp in range(2):
                    last = pool.memset(kh[N * hp:N * hp + N, :, :, :, N * hp + C:N * hp + C + 1], 1.0)
                last.then_inc(s_zero, 1)
                pool.drain()
                for t in range(2, STRIPS):
                    if t >= DEEP:
                        pool.wait_ge(s_pt, (s * STRIPS + t - DEEP + 1) * QUARTERS)
                    if t == STRIPS - 1:
                        pool.memset(strip[:, t % DEEP, :, LAST_W + 1:PW], 0.0)
                    norm_strip(pool, s_next, s, t, t % DEEP, 0, PW if t < STRIPS - 1 else LAST_W + 1)
                coefficients(2)
                stage_end(pool, s, 2)
                stage_end(pool, s, 3)
                with pool.Fori(0, NWIN) as w1:
                    half = NWIN // 2
                    for hf in range(2):
                        pool.wait_ge(s_xg if hf else s_xb, slot(s * NWIN + w1))
                        pool.tensor_tensor(
                            qb[:, hf, :, :, :].rearrange("p q j i -> p q (j i)"),
                            c("bq").rearrange("p (o n) -> p o n", o=1).broadcast_to([P, half, N]),
                            ksum[:, ds(w1 * NWIN + hf * half, half)].rearrange("p (q o) -> p q o", o=1
                                                                               ).broadcast_to([P, half, N]),
                            ALU.mult).then_inc(s_qb, 1)
                    pool.wait_ge(s_qb, s * NB + w1 * 2 + 2)
                    v = X3[:, ds(s * W + w1 * WS, WS), half * WS:2 * half * WS].rearrange("p j (q i) -> p j q i", i=WS)
                    pool.tensor_tensor(v, v, qb[:, 1, :, :, :].rearrange("p q j i -> p j q i"), ALU.add
                                       ).then_inc(s_xg, 1)
                coefficients(3)
                assert cnt[0] == PS
                stage_end(pool, s, 4)
                stage_end(pool, s, 5)
                stage_end(pool, s, 6)
                with pool.Fori(0, 8) as i:
                    for u in range(1, DEEP, 2):
                        pool.wait_ge(s_so, i * 2 + after(s * (NB // 2) + u // 2))
                        pool.tensor_tensor(vb[:, u, :], xd[:, u // 2, :], vb[:, u, :], ALU.mult).then_inc(s_v[1], 1)
                stage_end(pool, s, 7)
            va = vall[:, :].rearrange("p (s k) -> p k s", k=4)
            pool.tensor_tensor(bns[:, 0:2], va[:, 0, :], va[:, 2, :], ALU.mult).then_inc(s_g, 1)
            pool.tensor_tensor(bns[:, 2:4], va[:, 1, :], va[:, 2, :], ALU.mult)
            pool.drain()
            pool.tensor_tensor(bns[:, 2:4], bns[:, 2:4], va[:, 2, :], ALU.mult).then_inc(s_g, 1)
            pool.wait_ge(s_g, 9)
            pool.tensor_tensor(bns[:, 10:11], bns[:, 9:10], c("bn_eps"), ALU.add).then_inc(s_g, 1)
            pool.wait_ge(s_g, 10)
            pool.tensor_tensor(bns[:, 10:11], bns[:, 10:11], c("root"), ALU.pow).then_inc(s_g, 1)
            with pool.Fori(0, NS) as s:
                with pool.Fori(0, NB // ROWS) as i:
                    for u in range(ROWS):
                        n = i * ROWS + u
                        pool.wait_ge(s_fl, s * NB + i * ROWS + (u + 1))
                        pool.tensor_tensor(rows4(row[:, u, :]), columns(s, n), rows4(row[:, u, :]), ALU.add
                                           ).then_inc(s_fo, 1)


def constants(w1, wg, w2, fir, W_qk, b_qk, temperature, W9, b9, gamma, beta):
    t = np.zeros((P, NCONST), np.float32)

    def put(name, a):
        at, n = AT[name]
        t[:, at:at + n] = np.asarray(a, np.float32).reshape(P, n)

    put("ident", np.eye(P))
    a = np.zeros((G, C, MULTI, G, C), np.float32)
    for j in range(G):
        a[j, :, :, j] = wg.transpose(2, 0, 1)
    put("wg", a)
    put("w2", np.tile(w2, (G, 1)))
    a = np.zeros((PH, PW, OW, OH), np.float32)
    for h in range(PH):
        for w in range(PW):
            for j in range(max(0, w - TAPS + 1), min(OW, w + 1)):
                a[h, w, j, h:h + TAPS] = fir[::-1, w - j]
    put("fir", a)
    a = np.zeros((G, C, G, C), np.float32)
    for g in range(G):
        a[g, :, g] = W_qk[N * HEADS:].T
    put("wk", a)
    heads = np.repeat(temperature, CK)
    put("temp", np.broadcast_to(np.tile(heads, G), (P, P)))
    put("bk", np.broadcast_to(np.tile(b_qk[N * HEADS:], G), (P, P)))
    put("bkc", np.tile(b_qk[N * HEADS:], G))
    put("tempc", np.tile(heads, G))
    q = W_qk[:N * HEADS].reshape(HEADS, WS, WS, C).transpose(3, 0, 2, 1)
    put("wq", np.broadcast_to(q[None], (G, C, HEADS, WS, WS)))
    bq = b_qk[:N * HEADS].reshape(HEADS, WS, WS).transpose(0, 2, 1).reshape(HEADS, N)
    put("bq", np.tile(np.repeat(bq, CK, axis=0), (G, 1)))
    a = np.zeros((G, C, COLS), np.float32)
    for g in range(G):
        a[g, :, g * K9:(g + 1) * K9] = W9
    put("w9", a)
    put("b9", np.broadcast_to(np.tile(b9, G), (P, G * K9)))
    a = np.zeros((P, 3, P), np.float32)
    for k in range(3):
        for h in range(1, H - 1):
            a[h, k, h + k - 1] = 1
    put("shift", a)
    put("mean8", np.tile(np.eye(C), (G, G)) / B)
    put("w1", np.tile(w1, (G, 1)))
    put("gamma", np.tile(gamma, G))
    put("beta", np.tile(beta, G))
    for name, v in (("gn_eps", GN_EPS), ("bn_eps", BN_EPS), ("root", -0.5), ("minus", -1.0)):
        put(name, np.full(P, v))
    return t


def kernel(x, L0_conv_w1, L0_conv_wg, L0_conv_w2, L1_conv_kernel, L2_conv_W_qk, L2_conv_b_qk, L2_conv_temperature,
           L3_conv_W1, L3_conv_b1, L3_conv_gamma, L3_conv_beta):
    import concourse.bacc as bacc
    from concourse.bass_utils import run_bass_kernel_spmd

    weights = [np.asarray(a) for a in (
        L0_conv_w1, L0_conv_wg, L0_conv_w2, L1_conv_kernel, L2_conv_W_qk, L2_conv_b_qk, L2_conv_temperature,
        L3_conv_W1, L3_conv_b1, L3_conv_gamma, L3_conv_beta)]
    choose = np.zeros((W // 4, G, W // 4, G, C), np.float32)
    for w in range(W // 4):
        for g in range(G):
            choose[w, g, w, g] = 1
    arrays = {"x": np.ascontiguousarray(x), "consts": constants(*weights), "choose": choose.reshape(P, W // 4, P)}
    nc = bacc.Bacc("TRN2", target_bir_lowering=False, num_devices=1)
    ins = [nc.dram_tensor(k, a.shape, mybir.dt.float32, kind="ExternalInput").ap() for k, a in arrays.items()]
    out = nc.dram_tensor("out", (B, H, W, C), mybir.dt.float32, kind="ExternalOutput").ap()
    build(nc, *ins, out)
    return run_bass_kernel_spmd(nc, [arrays], core_ids=[0]).results[0]["out"]
```
